# Optimizing a Trainium2 kernel written in Bass

```python
import numpy as np
import jax
import jax.numpy as jnp

def _softmax(x, axis=-1):
    return jax.nn.softmax(x, axis=axis)

def _gelu(x):
    return jax.nn.gelu(x, approximate=True)

def _silu(x):
    return jax.nn.silu(x)

def _sigmoid(x):
    return jax.nn.sigmoid(x)

def _layernorm(x, axis=-1, eps=1e-05):
    m = jnp.mean(x, axis=axis, keepdims=True)
    v = jnp.var(x, axis=axis, keepdims=True)
    return (x - m) / jnp.sqrt(v + eps)

def _scatter_add(tgt, idx, src, axis=0):
    return tgt.at[idx].add(src)

def _segment_sum(src, seg, n):
    return jax.ops.segment_sum(src, seg, n)
kernel_name = 'mk_flamingo_gated_d1_seqx_r4_44239e'

def setup_inputs(seed: int=0):
    np.random.seed(seed)
    _w = jnp.asarray

    def _rec_inputs():
        import jax
        import jax.numpy as jnp
        _rk = jax.random.key(seed)
        x = -0.0002928 + 1 * jax.random.normal(jax.random.fold_in(_rk, 1), (16, 128, 256), jnp.float32)
        _lenS = 128 - jax.random.randint(jax.random.fold_in(_rk, 7), (16,), 0, max(1, 128 // 4) + 1, jnp.int32)
        _lenS2 = 128 - jax.random.randint(jax.random.fold_in(_rk, 8), (16,), 0, max(1, 128 // 4) + 1, jnp.int32)
        _ctx_1024P = jax.random.normal(jax.random.fold_in(_rk, 11), (16, 16, 256), jnp.float32)
        _ctx_1024c = jax.random.dirichlet(jax.random.fold_in(_rk, 511), 0.3 * jnp.ones((16,), jnp.float32), (16, 128))
        _ctx_1024t = jnp.einsum('bsk,bkd->bsd', _ctx_1024c, _ctx_1024P)
        _ctx_1024t = _ctx_1024t * jax.lax.rsqrt(jnp.mean(jnp.square(_ctx_1024t)) + 1e-12) * 0.953939
        ctx_1024 = -1.39393e-06 + 0.999914 * (_ctx_1024t + 0.3 * jax.random.normal(jax.random.fold_in(_rk, 611), (16, 128, 256), jnp.float32))
        _g = jax.random.normal(jax.random.fold_in(_rk, 9001), (2, 1), jnp.float32)
        _g = jnp.sign(_g) * jnp.maximum(jnp.abs(_g), 1.0) + (_g == 0) * 1.0
        g_xattn = _g[0]
        g_ffn = _g[1]
        return (x, ctx_1024, g_xattn, g_ffn)
    x, ctx_1024, g_xattn, g_ffn = _rec_inputs()

    def _L0_xattn_setup():
        import jax, jax.numpy as jnp
        import numpy as np
        import math
        HIDDEN = 256
        HEADS = 16
        HEAD = HIDDEN // HEADS
        SCALE_BASE = 512.0

        def _gammas(heads):
            return 1.0 - jnp.exp(jnp.linspace(math.log(1.0 / 32.0), math.log(1.0 / 512.0), heads))

        def _xpos(x, downscale):
            S, d = (x.shape[2], x.shape[3])
            half = d // 2
            base_scale = (jnp.arange(0, d, 2, dtype=jnp.float32) + 0.4 * d) / (1.4 * d)
            pos = jnp.arange(S, dtype=jnp.float32)
            scale = base_scale[None, :] ** (pos / SCALE_BASE)[:, None]
            if downscale:
                scale = 1.0 / scale
            inv_freq = 1.0 / 10000.0 ** (jnp.arange(half, dtype=jnp.float32) / half)
            sinusoid = pos[:, None] * inv_freq[None, :]
            sin = jnp.repeat(jnp.sin(sinusoid) * scale, 2, axis=-1)
            cos = jnp.repeat(jnp.cos(sinusoid) * scale, 2, axis=-1)
            x1 = x[..., ::2]
            x2 = x[..., 1::2]
            rot = jnp.stack([-x2, x1], axis=-1).reshape(x.shape)
            return x * cos + rot * sin

        def _decay_mask(S, gammas):
            n = jnp.arange(S)[:, None]
            m = jnp.arange(S)[None, :]
            diff = (n - m).astype(jnp.float32)
            mask = n >= m
            pw = jnp.maximum(diff, 0.0)[None, :, :]
            return jnp.where(mask[None, :, :], gammas[:, None, None] ** pw, 0.0)

        def retention_forward(Q, K, V):
            B, S, _ = Q.shape

            def split(x, hd):
                return x.reshape(B, S, HEADS, hd).transpose(0, 2, 1, 3)
            q = _xpos(split(Q, HEAD), downscale=False)
            k = _xpos(split(K, HEAD), downscale=True)
            v = split(V, HEAD)
            D = _decay_mask(S, _gammas(HEADS).astype(Q.dtype))
            scores = jnp.einsum('bhsd,bhtd->bhst', q, k) * D[None]
            out = jnp.einsum('bhst,bhtd->bhsd', scores, v)
            return out.transpose(0, 2, 1, 3).reshape(B, S, HEADS * HEAD)
        key = jax.random.key(seed)
        kq, kk, kv = jax.random.split(key, 3)
        B, S = (2, 512)
        return {'Q': jax.random.normal(kq, (B, S, HIDDEN), dtype=jnp.float32), 'K': jax.random.normal(kk, (B, S, HIDDEN), dtype=jnp.float32), 'V': jax.random.normal(kv, (B, S, HIDDEN), dtype=jnp.float32)}
    _L0_xattn_all = _L0_xattn_setup()
    _L0_xattn_in = {k: v for k, v in _L0_xattn_all.items() if k in ()}
    del _L0_xattn_all

    def _L0_ffn_setup():
        import jax, jax.numpy as jnp
        import numpy as np
        EMBED_DIM = 256
        HIDDEN_DIM = 1024
        NUM_EXPERTS = 8
        TOP_K = 2
        key = jax.random.key(seed)
        ks = jax.random.split(key, 6)
        B, S, D, H, E = (2, 512, EMBED_DIM, HIDDEN_DIM, NUM_EXPERTS)
        x = jax.random.normal(ks[0], (B, S, D), dtype=jnp.float32)
        router_w = jax.random.normal(ks[1], (D, E), dtype=jnp.float32) * (1.0 / np.sqrt(D))
        w1 = jax.random.normal(ks[2], (E, D, H), dtype=jnp.float32) * (1.0 / np.sqrt(D))
        b1 = jnp.zeros((E, H), dtype=jnp.float32)
        w2 = jax.random.normal(ks[3], (E, H, D), dtype=jnp.float32) * (1.0 / np.sqrt(H))
        b2 = jnp.zeros((E, D), dtype=jnp.float32)
        return {'x': x, 'router_w': router_w, 'w1': w1, 'b1': b1, 'w2': w2, 'b2': b2}
    _L0_ffn_all = _L0_ffn_setup()
    _L0_ffn_in = {k: v for k, v in _L0_ffn_all.items() if k in ('router_w', 'w1', 'b1', 'w2', 'b2')}
    del _L0_ffn_all
    return {'x': x, 'ctx_1024': ctx_1024, 'g_xattn': g_xattn, 'g_ffn': g_ffn, 'L0_ffn_router_w': _L0_ffn_in['router_w'], 'L0_ffn_w1': _L0_ffn_in['w1'], 'L0_ffn_b1': _L0_ffn_in['b1'], 'L0_ffn_w2': _L0_ffn_in['w2'], 'L0_ffn_b2': _L0_ffn_in['b2']}

def reference(x, ctx_1024, g_xattn, g_ffn, L0_ffn_router_w, L0_ffn_w1, L0_ffn_b1, L0_ffn_w2, L0_ffn_b2):
    import jax
    import jax.numpy as jnp

    def _L0_xattn_ref(Q, K, V):
        import jax, jax.numpy as jnp
        import numpy as np
        import math
        HIDDEN = 256
        HEADS = 16
        HEAD = HIDDEN // HEADS
        SCALE_BASE = 512.0

        def _gammas(heads):
            return 1.0 - jnp.exp(jnp.linspace(math.log(1.0 / 32.0), math.log(1.0 / 512.0), heads))

        def _xpos(x, downscale):
            S, d = (x.shape[2], x.shape[3])
            half = d // 2
            base_scale = (jnp.arange(0, d, 2, dtype=jnp.float32) + 0.4 * d) / (1.4 * d)
            pos = jnp.arange(S, dtype=jnp.float32)
            scale = base_scale[None, :] ** (pos / SCALE_BASE)[:, None]
            if downscale:
                scale = 1.0 / scale
            inv_freq = 1.0 / 10000.0 ** (jnp.arange(half, dtype=jnp.float32) / half)
            sinusoid = pos[:, None] * inv_freq[None, :]
            sin = jnp.repeat(jnp.sin(sinusoid) * scale, 2, axis=-1)
            cos = jnp.repeat(jnp.cos(sinusoid) * scale, 2, axis=-1)
            x1 = x[..., ::2]
            x2 = x[..., 1::2]
            rot = jnp.stack([-x2, x1], axis=-1).reshape(x.shape)
            return x * cos + rot * sin

        def _decay_mask(S, gammas):
            n = jnp.arange(S)[:, None]
            m = jnp.arange(S)[None, :]
            diff = (n - m).astype(jnp.float32)
            mask = n >= m
            pw = jnp.maximum(diff, 0.0)[None, :, :]
            return jnp.where(mask[None, :, :], gammas[:, None, None] ** pw, 0.0)

        def retention_forward(Q, K, V):
            B, S, _ = Q.shape

            def split(x, hd):
                return x.reshape(B, S, HEADS, hd).transpose(0, 2, 1, 3)
            q = _xpos(split(Q, HEAD), downscale=False)
            k = _xpos(split(K, HEAD), downscale=True)
            v = split(V, HEAD)
            D = _decay_mask(S, _gammas(HEADS).astype(Q.dtype))
            scores = jnp.einsum('bhsd,bhtd->bhst', q, k) * D[None]
            out = jnp.einsum('bhst,bhtd->bhsd', scores, v)
            return out.transpose(0, 2, 1, 3).reshape(B, S, HEADS * HEAD)
        return retention_forward(Q, K, V)

    def _L0_ffn_ref(x, router_w, w1, b1, w2, b2):
        import jax, jax.numpy as jnp
        import numpy as np
        EMBED_DIM = 256
        HIDDEN_DIM = 1024
        NUM_EXPERTS = 8
        TOP_K = 2
        logits = jnp.einsum('bsd,de->bse', x, router_w)
        probs = jax.nn.softmax(logits, axis=-1)
        weights, idx = jax.lax.top_k(probs, TOP_K)
        weights = weights / jnp.sum(weights, axis=-1, keepdims=True)
        dispatch = jnp.sum(jax.nn.one_hot(idx, NUM_EXPERTS, dtype=x.dtype) * weights[..., None], axis=-2)
        h = jnp.einsum('bsd,edh->besh', x, w1) + b1[None, :, None, :]
        h = jax.nn.gelu(h, approximate=False)
        out_e = jnp.einsum('besh,ehd->besd', h, w2) + b2[None, :, None, :]
        out = jnp.einsum('besd,bse->bsd', out_e, dispatch)
        return out
    x = x + jnp.tanh(g_xattn[0]) * _L0_xattn_ref(_layernorm(x, axis=-1), ctx_1024, ctx_1024)
    x = x + jnp.tanh(g_ffn[0]) * _L0_ffn_ref(_layernorm(x, axis=-1), L0_ffn_router_w, L0_ffn_w1, L0_ffn_b1, L0_ffn_w2, L0_ffn_b2)
    return x

_drawn_inputs = setup_inputs


def setup_inputs(seed=0):
    import zlib

    import numpy as np

    out = dict(_drawn_inputs(seed))
    spreads = {'L0_ffn_b1': (0.0, 0.8), 'L0_ffn_b2': (0.0, 2.0)}
    factors = {'L0_ffn_router_w': 7.093, 'L0_ffn_w1': 6.986, 'L0_ffn_w2': 6.296}
    for name, (base, spread) in spreads.items():
        noise = np.random.default_rng([zlib.crc32(name.encode()), seed]).standard_normal(out[name].shape)
        drawn = base * np.exp(spread * noise) if base else spread * noise
        out[name] = jnp.asarray(drawn.astype(out[name].dtype))
    for name, factor in factors.items():
        out[name] = (out[name] * factor).astype(out[name].dtype)
    return out
```

```python
import math
from contextlib import ExitStack

import numpy as np

import concourse.bass as bass
from concourse import mybir

ALU = mybir.AluOpType
ACT = mybir.ActivationFunctionType
AX = mybir.AxisListType
F32 = mybir.dt.float32
BF16 = mybir.dt.bfloat16
I32 = mybir.dt.int32
U32 = mybir.dt.uint32

P = 128
B, S, D = 16, 128, 256
HEADS, HD = 16, 16
E, H, TOPK = 8, 1024, 2
TOKENS = B * S
DC = D // P
HC = H // P
ROWS = 2 * P
TILES = TOKENS * TOPK // ROWS + E - 1
TCOLS = 2 * TILES + 2
EPS = 1e-5
SLOTS = 4
HOT = 4
SPARE = P

CQ, SQ, CK, SK = 0, D, 2 * D, 3 * D
IDENT = 4 * D
CAUSAL = IDENT + P
IOTA = CAUSAL + P
TOKEN1 = IOTA + P
SPARE1 = TOKEN1 + B
BELOW8 = SPARE1 + 1
NCONST = BELOW8 + E
IDENT_B, BEFORE_B, ONES_B, NCONST_B = 0, P, 2 * P, 3 * P


def constants():
    half = HD // 2
    base = (np.arange(0, HD, 2, dtype=np.float32) + np.float32(0.4 * HD)) / np.float32(1.4 * HD)
    pos = np.arange(S, dtype=np.float64)
    scale = base.astype(np.float64)[None, :] ** (pos / 512.0)[:, None]
    freq = (1.0 / 10000.0 ** (np.arange(half, dtype=np.float32) / np.float32(half))).astype(np.float32)
    angle = (pos[:, None].astype(np.float32) * freq[None, :]).astype(np.float64)
    gamma = (1.0 - np.exp(np.linspace(math.log(1 / 32), math.log(1 / 512), HEADS))).astype(np.float32)
    decay = gamma.astype(np.float64)[None, :] ** pos[:, None]
    c = np.zeros((P, NCONST), np.float32)
    for at_cos, at_sin, factor in ((CQ, SQ, decay[:, :, None] * scale[:, None, :]),
                                   (CK, SK, 1 / (decay[:, :, None] * scale[:, None, :]))):
        cos = np.cos(angle)[:, None, :] * factor
        sin = np.sin(angle)[:, None, :] * factor
        c[:, at_cos:at_cos + D] = np.stack([cos, cos], -1).reshape(S, D)
        c[:, at_sin:at_sin + D] = np.stack([-sin, sin], -1).reshape(S, D)
    c[:, IDENT:IDENT + P] = np.eye(P)
    c[:, CAUSAL:CAUSAL + P] = np.triu(np.ones((P, P)))
    c[:, IOTA:IOTA + P] = np.arange(P)
    c[:, TOKEN1:TOKEN1 + B] = 1 + np.arange(P)[:, None] + P * np.arange(B)
    c[:, SPARE1] = 1 + TOKENS + np.arange(P)
    c[:, BELOW8:BELOW8 + E] = np.arange(E) - E
    cb = np.zeros((P, NCONST_B), np.float32)
    cb[:, IDENT_B:IDENT_B + P] = np.eye(P)
    cb[:, BEFORE_B:BEFORE_B + P] = np.triu(np.ones((P, P)), 1)
    cb[:, ONES_B:ONES_B + P] = 1
    return c, cb


def swapped(ap):
    return ap.rearrange("p (a b) -> p a b", b=2)[:, :, ::-1]


def pairs(ap):
    return ap.rearrange("p (a b) -> p a b", b=2)


def build(nc, x, ctx, gates, router_w, w1, b1, w2, b2, const, const_b, out):
    with ExitStack() as stack:
        def sb(name, shape, dt):
            return stack.enter_context(nc.sbuf_tensor(name, shape, dt))

        def psum(name, shape, dt=F32):
            return stack.enter_context(nc.psum_tensor(name, shape, dt))

        def sem(name):
            return stack.enter_context(nc.semaphore(name))

        def sem2(name):
            return [sem(f"{name}{par}") for par in range(2)]

        x_rows = x.rearrange("b s d -> (b s) d")
        ctx_rows = ctx.rearrange("b s d -> (b s) d")
        w1_rows = w1.rearrange("e d h -> (e d) h")
        w2_rows = w2.rearrange("e h d -> (e h) d")
        normed_dram = nc.dram_tensor("normed_rows", [TOKENS, 2 * D], BF16, kind="Internal").ap()

        cst = sb("cst", [P, NCONST], F32)
        cstb = sb("cstb", [P, NCONST_B], BF16)
        gate = sb("gate", [P, 2], F32)
        minus_half = sb("minus_half", [P, 2], F32)
        rw = sb("rw", [P, DC, E], F32)
        b1c = sb("b1c", [P, E * HC], F32)
        zero_rows = sb("zero_rows", [P, D], F32)
        w1s = sb("w1s", [P, E * 2 * DC * H], BF16)
        w2s = sb("w2s", [P, E * 2 * HC * D], BF16)
        raw = sb("raw", [P, 4 * H], F32)
        raw1 = [raw[:, par * H:(par + 1) * H] for par in range(2)]
        raw2 = [raw[:, (2 + par) * H:(3 + par) * H] for par in range(2)]
        b2bc = raw[:, 0:E * D]
        act32 = raw[:, E * D:E * D + HC * ROWS]

        seq_in = sb("seq_in", [P, SLOTS * D], F32)
        context = sb("context", [P, SLOTS, D + HD], F32)
        xin = [seq_in[:, s * D:(s + 1) * D] for s in range(SLOTS)]
        cin = [context[:, s, 0:D] for s in range(SLOTS)]
        stats = sb("stats", [P, 6], F32)
        moments = sb("moments", [P, 2, 2], F32)
        mean1, mean2 = moments[:, 0, :], moments[:, 1, :]
        veps = sb("veps", [P, 2], F32)
        rstd = sb("rstd", [P, 2], F32)
        rotary = sb("rotary", [P, 5 * D], F32)
        xn, turn, kturn, qrot, krot = (rotary[:, n * D:(n + 1) * D] for n in range(5))
        ksplit = sb("ksplit", [P, HEADS, 2, HD], BF16)
        qhi = sb("qhi", [P, HEADS, 2, HD], BF16)
        qlo = sb("qlo", [P, HEADS, 2, HD], BF16)
        kqT = sb("kqT", [P, 3, 4, P], BF16)
        masked = sb("masked", [P, 4 * 4 * P], F32)
        smask = [masked[:, 4 * j * P:4 * (j + 1) * P].rearrange("p (g n) -> p g n", g=4) for j in range(4)]
        halves = masked[:, 0:NCONST_B]
        stats2 = sb("stats2", [P, 6], F32)
        x2n = sb("x2n", [P, D], F32)
        x2split = [sb(f"x2split{s}", [P, 2 * D], BF16) for s in range(SLOTS)]
        x2T = sb("x2T", [P, DC, P], F32)
        outT = sb("outT", [P, 4 * P], F32)

        logits = sb("logits", [P, B * E], F32)
        others = sb("others", [P, B * E], F32)
        ties = sb("ties", [P, B * E], F32)
        first = sb("first", [P, B], F32)
        best = sb("best", [P, TOPK, B], F32)
        onehot = sb("onehot", [P, TOPK, B, E], F32)
        chosen = sb("chosen", [P, B + 1, E], BF16)
        count_i = sb("count_i", [P, E], I32)
        tiles_i = sb("tiles_i", [P, E], I32)
        tiles_f = sb("tiles_f", [P, E], F32)
        ends = sb("ends", [P, E], F32)
        starts = sb("starts", [P, E], F32)
        slot = sb("slot", [P, B, E], F32)
        slot_k = sb("slot_k", [P, TOPK, B, E], F32)
        slots = sb("slots", [P, TOPK * B], F32)
        slots_i = sb("slots_i", [P, TOPK * B], I32)
        tile_i = sb("tile_i", [P, TOPK * B], I32)
        tile_f = sb("tile_f", [P, TOPK * B], F32)
        lane_f = sb("lane_f", [P, TOPK * B], F32)
        gap = sb("gap", [P, B], F32)
        ratio = sb("ratio", [P, B], F32)
        total = sb("total", [P, B], F32)
        inverse = sb("inverse", [P, B], F32)
        weight = sb("weight", [P, TOPK * B], F32)
        lane_hot = [sb(f"lane_hot{n}", [P, P], F32) for n in range(HOT)]
        tile_hot = [sb(f"tile_hot{n}", [P, 2, TCOLS], F32) for n in range(HOT)]
        table = sb("table", [P, 2, TCOLS], F32)
        slot_gate = table[:, 1, :]
        row_less1 = sb("row_less1", [P, TCOLS], F32)
        empty = sb("empty", [P, TCOLS], F32)
        gather_row = sb("gather_row", [P, TCOLS], I32)
        scatter_row = sb("scatter_row", [P, TCOLS], I32)
        gather_now = [[sb(f"gather_now{p}{half}", [P, 1], I32) for half in range(2)] for p in range(2)]
        scatter_now = [sb(f"scatter_now{half}", [P, 1], I32) for half in range(2)]
        tile_ge = sb("tile_ge", [1, TCOLS, E], F32)
        tile_exp = sb("tile_exp", [1, TCOLS], F32)
        tile_expert = sb("tile_expert", [1, TCOLS], I32)

        rows_in = [seq_in[:, 2 * p * D:2 * (p + 1) * D].bitcast(BF16).rearrange("p (h d) -> p h d", h=2)
                   for p in range(2)]
        rowsT = [rotary[:, 2 * p * D:2 * (p + 1) * D].bitcast(BF16).rearrange("p (s c n) -> p s c n", s=2, c=DC)
                 for p in range(2)]
        gelu_even = sb("gelu_even", [P, 2, HC, ROWS], BF16)
        gelu_odd = masked[:, :].bitcast(BF16).rearrange("p (s c n) -> p s c n", s=2, c=HC)
        ghi = [gelu_even[:, 0, :, :], gelu_odd[:, 0, :, :]]
        glo = [gelu_even[:, 1, :, :], gelu_odd[:, 1, :, :]]
        ysum = [cin[half] for half in range(2)]
        yout = [cin[2 + half] for half in range(2)]

        bank = [psum(f"bank{n}", [P, 512]) for n in range(8)]
        sc_ps = bank[0:4]
        kq_ps = bank[4][:, :].bitcast(BF16)
        ql_ps = bank[5][:, :].bitcast(BF16)
        outT_ps = bank[0]
        o_ps = bank[6]
        r_ps = bank[7]
        logit_ps = r_ps[:, D:D + E]
        rank_ps = bank[0]
        table_ps = bank[1]
        h_ps = bank[0:4]
        t_ps = bank[4][:, :].bitcast(BF16)
        y_ps = [bank[5], bank[6]]

        const_in, gates_in, b2_in = sem("const_in"), sem("gates_in"), sem("b2_in")
        zeros_set, zeros_out = sem("zeros_set"), sem("zeros_out")
        half_set, gates_ready, halves_ok = sem("half_set"), sem("gates_ready"), sem("halves_ok")
        halves_in = sem("halves_in")
        xc_in, raw_in = [sem(f"xc_in{s}") for s in range(SLOTS)], sem2("raw_in")
        stats1_ok, mean1_ok, stats2_ok, mean2_ok = sem("stats1_ok"), sem("mean1_ok"), sem("stats2_ok"), sem("mean2_ok")
        veps_ok, rstd_ok = sem("veps_ok"), sem("rstd_ok")
        kterms, krot_ok, khi_ok, k_ok = sem("kterms"), sem("krot_ok"), sem("khi_ok"), sem("k_ok")
        xn_ok, qterms, qrot_ok, qhi_ok, q_ok = sem("xn_ok"), sem("qterms"), sem("qrot_ok"), sem("qhi_ok"), sem("q_ok")
        kqT_made, kqT_ok, qlT_ok = sem("kqT_made"), sem("kqT_ok"), sem("qlT_ok")
        score_made = sem("score_made")
        s0_ok, copied, selected = sem("s0_ok"), sem("copied"), sem("selected")
        pads_set, outT_made, outT_ok, out_made = sem("pads_set"), sem("outT_made"), sem("outT_ok"), sem("out_made")
        x1_ok = sem("x1_ok")
        x1_out, x2_out = sem2("x1_out"), sem2("x2_out")
        x2n_ok, x2hi_ok, x2lo_ok = sem("x2n_ok"), sem("x2hi_ok"), sem("x2lo_ok")
        x2T_made, x2T_ok, logit_made, logit_ok = sem("x2T_made"), sem("x2T_ok"), sem("logit_made"), sem("logit_ok")
        w1hi_ok, w1lo_ok, w2hi_ok, w2lo_ok = sem("w1hi_ok"), sem("w1lo_ok"), sem("w2hi_ok"), sem("w2lo_ok")
        route_step, chosen_ok, rank_made = sem("route_step"), sem("chosen_ok"), sem("rank_made")
        gap_ok, ratio_ok = sem("gap_ok"), sem("ratio_ok")
        hot_ok, hot_used = sem("hot_ok"), sem("hot_used")
        experts_ok, slots_ok = sem("experts_ok"), sem("slots_ok")
        gathered, scattered = sem2("gathered"), sem2("scattered")
        gather_set, scatter_set = sem("gather_set"), sem("scatter_set")
        rowsT_made, rowsT_ok = sem("rowsT_made"), sem("rowsT_ok")
        h_made, gelu_ok, ghi_ok, glo_ok = sem("h_made"), sem("gelu_ok"), sem("ghi_ok"), sem("glo_ok")
        y_made, ysum_ok, yout_ok = sem("y_made"), sem("ysum_ok"), sem("yout_ok")

        block = stack.enter_context(nc.Block())

        def over_sequences(step):
            def run(eng):
                for n in range(-2, 2):
                    step(0, n)
                with eng.Fori(0, B // SLOTS - 1) as i:
                    for n in range(2, 2 + SLOTS):
                        step(i, n)
                for n in range(B - 2, B + 2):
                    step(0, n)
            return run

        def real(i, n):
            return not isinstance(i, int) or 0 <= n < B

        def num(i, n):
            return SLOTS * i + n

        def half_num(i, n):
            return SLOTS // 2 * i + n // 2

        def following(t, k, par):
            return t + 1, (k + 1 if par else k), 1 - par

        def w1_at(i, n):
            return half_num(i, n) * (2 * DC * H) + n % 2 * H

        def w2_at(i, n):
            return half_num(i, n) * (2 * HC * D) + n % 2 * H

        def own(eng, sem, value):
            if not isinstance(value, int):
                value = eng.lower_val(value)
            eng.wait_ge(const_in, 48)
            eng.wait_ge(sem, value)

        def is_first(t):
            return isinstance(t, int) and t == 0

        def over_tiles(eng, step):
            step(0, 0, 0)
            step(1, 0, 1)
            with eng.Fori(1, TILES // 2 - 1) as i:
                step(2 * i, i, 0)
                step(2 * i + 1, i, 1)
            for t in range(TILES - 3, TILES):
                step(t, t // 2, t % 2)

        @block.sync
        def _(sp):
            def load_seq(i, n):
                rows = bass.ds(num(i, n) * P, P)
                sp.dma_start(xin[n % SLOTS], x_rows[rows, :]).then_inc(xc_in[n % SLOTS], 16)
                sp.dma_start(cin[n % SLOTS], ctx_rows[rows, :]).then_inc(xc_in[n % SLOTS], 16)

            def load_raw(i, n):
                sp.dma_start(raw1[n % 2], w1_rows[bass.ds(num(i, n) * P, P), :]).then_inc(raw_in[n % 2], 16)
                sp.dma_start(raw2[n % 2].rearrange("p (c d) -> p c d", c=4),
                             w2_rows[bass.ds(num(i, n) * 4 * P, 4 * P), :].rearrange("(c p) d -> p c d", p=P)
                             ).then_inc(raw_in[n % 2], 16)

            load_seq(0, 0)
            sp.dma_start(cst[:, :], const).then_inc(const_in, 16)
            sp.dma_start(halves[:, :], const_b).then_inc(halves_in, 16)
            sp.dma_start(gate[:, :], gates.to_broadcast([P, 2])).then_inc(gates_in, 16)
            sp.dma_start(rw[:, :, :], router_w.rearrange("(c p) e -> p c e", p=P)).then_inc(const_in, 16)
            sp.dma_start(b1c[:, :], b1).then_inc(const_in, 16)
            load_seq(0, 1)
            load_raw(0, 0)
            load_seq(0, 2)
            load_raw(0, 1)
            load_seq(0, 3)
            sp.wait_ge(zeros_set, 1)
            sp.dma_start(out[TOKENS:TOKENS + SPARE, :], zero_rows[:, :]).then_inc(zeros_out, 16)

            def step(i, n):
                if real(i, n - 2):
                    if real(i, n + 2):
                        sp.wait_ge(x2n_ok, num(i, n - 1))
                        sp.wait_ge(x1_out[n % 2], 16 * half_num(i, n))
                        load_seq(i, n + 2)
                    sp.wait_ge(x2lo_ok, num(i, n - 1))
                    sp.dma_start(normed_dram[bass.ds(num(i, n - 2) * P, P), :],
                                 x2split[(n - 2) % SLOTS][:, :]).then_inc(x2_out[n % 2], 16)
                if real(i, n - 1):
                    sp.wait_ge(x1_ok, num(i, n))
                    sp.dma_start(out[bass.ds(num(i, n - 1) * P, P), :],
                                 xin[(n - 1) % SLOTS]).then_inc(x1_out[(n - 1) % 2], 16)
                    if real(i, n + 1):
                        if real(i, n - 2):
                            sp.wait_ge(x2_out[n % 2], 16 * half_num(i, n))
                        sp.wait_ge(w1lo_ok, num(i, n))
                        sp.wait_ge(w2lo_ok, num(i, n))
                        load_raw(i, n + 1)

            over_sequences(step)(sp)
            sp.wait_ge(w1lo_ok, B)
            sp.wait_ge(w2lo_ok, B)
            sp.dma_start(b2bc, b2.to_broadcast([P, E * D])).then_inc(b2_in, 16)
            sp.wait_ge(scattered[0], 16 * TILES)
            sp.wait_ge(scattered[1], 16 * TILES)

        @block.gpsimd
        def _(pool):
            pool.memset(zero_rows[:, :], 0.0).then_inc(zeros_set, 1)
            pool.memset(context[:, :, D:D + HD], 0.0).then_inc(pads_set, 1)
            pool.memset(minus_half[:, :], -0.5).then_inc(half_set, 1)
            pool.wait_ge(half_set, 1)

            def inverse_roots(i, n):
                one, two = real(i, n + 2), real(i, n - 1)
                columns = slice(0 if one else 1, 2 if two else 1)
                if one:
                    own(pool, mean1_ok, num(i, n + 3))
                if two:
                    own(pool, mean2_ok, num(i, n))
                pool.tensor_scalar(veps[:, columns], moments[:, columns, 1], EPS, None, ALU.add).then_inc(veps_ok, 1)
                pool.wait_ge(veps_ok, num(i, n + 3))
                pool.tensor_tensor(rstd[:, columns], veps[:, columns], minus_half[:, columns],
                                   ALU.pow).then_inc(rstd_ok, 1)

            def select(i, n, j):
                own(pool, copied, 3 * num(i, n) + j)
                pool.affine_select(out=smask[j], in_=smask[j], compare_op=ALU.is_ge, fill=0.0, base=0,
                                   pattern=[[0, 4], [1, P]], channel_multiplier=-1).then_inc(selected, 1)

            def step(i, n):
                if real(i, n):
                    select(i, n, 1)
                    select(i, n, 2)
                if real(i, n + 2) or real(i, n - 1):
                    inverse_roots(i, n)
                if real(i, n):
                    select(i, n, 3)
                    pool.wait_ge(w2hi_ok, num(i, n + 1))
                    at = w2_at(i, n)
                    pool.tensor_tensor(w2s[:, bass.ds(at + HC * D, H)], raw2[n % 2], w2s[:, bass.ds(at, H)],
                                       ALU.subtract).then_inc(w2lo_ok, 1)

            over_sequences(step)(pool)

            def gather(t, k, par):
                for half in range(2):
                    pool.tensor_copy(gather_now[par][half][:, :],
                                     gather_row[:, bass.ds(2 * t + half, 1)]).then_inc(gather_set, 1)
                    own(pool, gather_set, 2 * t + half + 1)
                    pool.indirect_dma_start(
                        out=rows_in[par][:, half, :], out_offset=None, in_=normed_dram,
                        in_offset=bass.IndirectOffsetOnAxis(ap=gather_now[par][half][:, :], axis=0),
                        bounds_check=TOKENS - 1).then_inc(gathered[par], 16)

            pool.wait_ge(slots_ok, 2)
            for par in range(2):
                pool.wait_ge(x2_out[par], 16 * (B // 2))
                pool.wait_ge(x1_out[par], 16 * (B // 2))
            pool.wait_ge(zeros_out, 16)
            gather(0, 0, 0)
            gather(1, 0, 1)
            pool.wait_ge(rowsT_made, 1)
            gather(2, 1, 0)

            def tile(t, k, par):
                if not (isinstance(t, int) and t >= TILES - 3):
                    pool.wait_ge(rowsT_made, t + 2)
                    gather(*following(t + 2, k + 1, par))
                for half in range(2):
                    pool.tensor_copy(scatter_now[half][:, :],
                                     scatter_row[:, bass.ds(2 * t + half, 1)]).then_inc(scatter_set, 1)
                    own(pool, scatter_set, 2 * t + half + 1)
                    pool.wait_ge(yout_ok, 2 * t + half + 1)
                    own(pool, scattered[1 - half], 16 * (t + half))
                    pool.indirect_dma_start(
                        out=out, out_offset=bass.IndirectOffsetOnAxis(ap=scatter_now[half][:, :], axis=0),
                        in_=yout[half], in_offset=None, bounds_check=TOKENS + SPARE - 1,
                        compute_op=ALU.add).then_inc(scattered[half], 16)

            over_tiles(pool, tile)

        @block.scalar
        def _(act):
            act.wait_ge(gates_in, 16)
            nc.scalar.activation(gate[:, :], gate[:, :], ACT.Tanh).then_inc(gates_ready, 1)
            act.wait_ge(halves_in, 16)
            nc.scalar.copy(cstb[:, :], halves[:, :]).then_inc(halves_ok, 1)

            def heads(ap):
                return ap.rearrange("p (h d) -> p h d", d=HD)

            def step(i, n):
                if real(i, n - 1):
                    act.wait_ge(outT_made, num(i, n))
                    if real(i, n - 2):
                        act.wait_ge(out_made, num(i, n - 1))
                    nc.scalar.copy(outT[:, :], outT_ps[:, :]).then_inc(outT_ok, 1)
                if real(i, n):
                    for j in range(1, 4):
                        act.wait_ge(score_made, 4 * num(i, n) + j)
                        nc.scalar.copy(smask[j], sc_ps[j][:, :]).then_inc(copied, 1)
                if real(i, n - 2):
                    act.wait_ge(x2T_made, num(i, n - 1))
                    nc.scalar.copy(x2T[:, :, :], r_ps[:, 0:D]).then_inc(x2T_ok, 1)
                if real(i, n + 1):
                    act.wait_ge(kqT_made, 2 * num(i, n + 1) + 1)
                    nc.scalar.copy(kqT[:, 0:2, :, :], kq_ps[:, 0:8 * P]).then_inc(kqT_ok, 1)
                    act.wait_ge(kqT_made, 2 * num(i, n + 2))
                    nc.scalar.copy(kqT[:, 2, :, :], ql_ps[:, 0:4 * P]).then_inc(qlT_ok, 1)
                if real(i, n):
                    act.wait_ge(raw_in[n % 2], 32 * (half_num(i, n) + 1))
                    nc.scalar.copy(w2s[:, bass.ds(w2_at(i, n), H)], raw2[n % 2]).then_inc(w2hi_ok, 1)
                if real(i, n + 2):
                    act.wait_ge(krot_ok, num(i, n + 3))
                    nc.scalar.copy(ksplit[:, :, 0, :], heads(krot)).then_inc(khi_ok, 1)
                if real(i, n):
                    nc.scalar.copy(w1s[:, bass.ds(w1_at(i, n), H)], raw1[n % 2]).then_inc(w1hi_ok, 1)
                if real(i, n - 1):
                    act.wait_ge(x2n_ok, num(i, n))
                    nc.scalar.copy(x2split[(n - 1) % SLOTS][:, 0:D], x2n[:, :]).then_inc(x2hi_ok, 1)
                if real(i, n + 2):
                    act.wait_ge(qrot_ok, num(i, n + 3))
                    nc.scalar.copy(qhi[:, :, :, :],
                                   heads(qrot).unsqueeze(2).to_broadcast([P, HEADS, 2, HD])).then_inc(qhi_ok, 1)

            over_sequences(step)(act)

            act.wait_ge(gap_ok, 1)
            nc.scalar.activation(ratio[:, :], gap[:, :], ACT.Exp).then_inc(ratio_ok, 1)

            act.wait_ge(experts_ok, 1)
            act.wait_ge(w1lo_ok, B)
            act.wait_ge(w2lo_ok, B)

            def tile(t, k, par):
                e = act.value_load(tile_expert[0:1, bass.ds(t, 1)], min_val=0, max_val=E - 1)
                for pair in range(4):
                    act.wait_ge(h_made, 4 * t + pair + 1)
                    if not is_first(t):
                        act.wait_ge(glo_ok, 4 * t + pair - 3)
                    for c in (2 * pair, 2 * pair + 1):
                        last = nc.scalar.activation(act32[:, c * ROWS:(c + 1) * ROWS],
                                                    h_ps[pair][:, c % 2 * ROWS:(c % 2 + 1) * ROWS],
                                                    ACT.Gelu, bias=b1c[:, bass.ds(e * HC + c, 1)])
                    last.then_inc(gelu_ok, 1)

            over_tiles(act, tile)

        @block.vector
        def _(dve):
            dve.wait_ge(const_in, 48)
            dve.wait_ge(gates_ready, 1)

            def statistics(count, data, stat, stat_ok, mean, mean_ok):
                nc.vector.bn_stats(stat[:, :], data).then_inc(stat_ok, 1)
                own(dve, stat_ok, count)
                nc.vector.bn_aggr(mean, stat[:, :]).then_inc(mean_ok, 1)

            def heads(ap):
                return ap.rearrange("p (h d) -> p h d", d=HD)

            def prepare_k(i, n):
                s = n % SLOTS
                nc.vector.tensor_tensor(krot, cin[s], cst[:, CK:CK + D], ALU.mult).then_inc(kterms, 1)
                nc.vector.tensor_tensor(pairs(kturn), swapped(cin[s]), pairs(cst[:, SK:SK + D]),
                                        ALU.mult).then_inc(kterms, 1)
                dve.wait_ge(kterms, 2 * num(i, n + 1))
                nc.vector.tensor_tensor(krot, krot, kturn, ALU.add).then_inc(krot_ok, 1)

            def prepare_q(i, n):
                s = n % SLOTS
                dve.wait_ge(rstd_ok, num(i, n + 1))
                nc.vector.tensor_scalar(xn, xin[s], mean1[:, 0:1], rstd[:, 0:1],
                                        ALU.subtract, ALU.mult).then_inc(xn_ok, 1)
                dve.wait_ge(xn_ok, num(i, n + 1))
                nc.vector.tensor_tensor(qrot, xn, cst[:, CQ:CQ + D], ALU.mult).then_inc(qterms, 1)
                nc.vector.tensor_tensor(pairs(turn), swapped(xn), pairs(cst[:, SQ:SQ + D]),
                                        ALU.mult).then_inc(qterms, 1)
                dve.wait_ge(qterms, 2 * num(i, n + 1))
                nc.vector.tensor_tensor(qrot, qrot, turn, ALU.add).then_inc(qrot_ok, 1)

            def split_kq(i, n):
                dve.wait_ge(khi_ok, num(i, n + 1))
                nc.vector.tensor_tensor(ksplit[:, :, 1, :], heads(krot), ksplit[:, :, 0, :],
                                        ALU.subtract).then_inc(k_ok, 1)
                dve.wait_ge(qhi_ok, num(i, n + 1))
                nc.vector.tensor_tensor(qlo[:, :, :, :], heads(qrot).unsqueeze(2).to_broadcast([P, HEADS, 2, HD]),
                                        qhi[:, :, :, :], ALU.subtract).then_inc(q_ok, 1)

            def step(i, n):
                last = (n - 1) % SLOTS
                if real(i, n + 2):
                    s = (n + 2) % SLOTS
                    dve.wait_ge(xc_in[s], 32 * (i + (n + 2) // SLOTS + 1))
                    statistics(num(i, n + 3), xin[s], stats, stats1_ok, mean1, mean1_ok)
                    prepare_k(i, n + 2)
                if real(i, n - 1):
                    dve.wait_ge(out_made, num(i, n))
                    by_head = xin[last].rearrange("p (h d) -> p h d", d=HD)
                    nc.vector.scalar_tensor_tensor(
                        out=by_head, in0=o_ps[:, :].rearrange("p (h d) -> p h d", d=32)[:, :, 0:HD],
                        scalar=gate[:, 0:1], in1=by_head, op0=ALU.mult, op1=ALU.add).then_inc(x1_ok, 1)
                    dve.wait_ge(x1_ok, num(i, n))
                    statistics(num(i, n), xin[last], stats2, stats2_ok, mean2, mean2_ok)
                if real(i, n):
                    dve.wait_ge(score_made, 4 * num(i, n) + 4)
                    nc.vector.tensor_tensor(smask[0], sc_ps[0][:, :].rearrange("p (g n) -> p g n", g=4),
                                            cst[:, CAUSAL:CAUSAL + P].unsqueeze(1).to_broadcast([P, 4, P]),
                                            ALU.mult).then_inc(s0_ok, 1)
                if real(i, n + 2):
                    prepare_q(i, n + 2)
                if real(i, n - 2):
                    dve.wait_ge(logit_made, num(i, n - 1))
                    nc.vector.tensor_copy(logits[:, bass.ds(num(i, n - 2) * E, E)],
                                          logit_ps).then_inc(logit_ok, 1)
                if real(i, n - 1):
                    dve.wait_ge(rstd_ok, num(i, n + 3))
                    if real(i, n - 2):
                        dve.wait_ge(x2T_made, num(i, n - 1))
                    nc.vector.tensor_scalar(x2n[:, :], xin[last], mean2[:, 0:1], rstd[:, 1:2],
                                            ALU.subtract, ALU.mult).then_inc(x2n_ok, 1)
                if real(i, n):
                    dve.wait_ge(w1hi_ok, num(i, n + 1))
                    at = w1_at(i, n)
                    nc.vector.tensor_tensor(w1s[:, bass.ds(at + DC * H, H)], raw1[n % 2], w1s[:, bass.ds(at, H)],
                                            ALU.subtract).then_inc(w1lo_ok, 1)
                if real(i, n - 1):
                    dve.wait_ge(x2hi_ok, num(i, n))
                    nc.vector.tensor_tensor(x2split[last][:, D:2 * D], x2n[:, :], x2split[last][:, 0:D],
                                            ALU.subtract).then_inc(x2lo_ok, 1)
                if real(i, n + 2):
                    split_kq(i, n + 2)

            over_sequences(step)(dve)

            steps = 0

            def then(ins):
                nonlocal steps
                steps += 1
                ins.then_inc(route_step, 1)
                dve.wait_ge(route_step, steps)

            def by_sequence(ap):
                return ap.rearrange("p (b e) -> p b e", e=E)

            def over_experts(ap):
                return ap.unsqueeze(2).to_broadcast([P, B, E])

            below8 = cst[:, BELOW8:BELOW8 + E].unsqueeze(1).to_broadcast([P, B, E])
            dve.wait_ge(logit_ok, B)
            for choice in range(TOPK):
                left = logits if choice == 0 else others
                then(nc.vector.tensor_reduce(best[:, choice, :], by_sequence(left[:, :]), AX.X, ALU.max))
                then(nc.vector.tensor_tensor(by_sequence(ties[:, :]), by_sequence(left[:, :]),
                                             over_experts(best[:, choice, :]), ALU.is_equal))
                then(nc.vector.tensor_tensor(by_sequence(ties[:, :]), by_sequence(ties[:, :]), below8, ALU.mult))
                then(nc.vector.tensor_reduce(first[:, :], by_sequence(ties[:, :]), AX.X, ALU.min))
                then(nc.vector.tensor_tensor(onehot[:, choice, :, :], below8, over_experts(first[:, :]),
                                             ALU.is_equal))
                if choice == 0:
                    then(nc.vector.scalar_tensor_tensor(
                        out=others[:, :], in0=onehot[:, 0, :, :].rearrange("p b e -> p (b e)"), scalar=-3e38,
                        in1=logits[:, :], op0=ALU.mult, op1=ALU.add))
            nc.vector.tensor_tensor(gap[:, :], best[:, 1, :], best[:, 0, :], ALU.subtract).then_inc(gap_ok, 1)
            nc.vector.memset(chosen[:, B, :], 0.0).then_inc(chosen_ok, 1)
            nc.vector.tensor_tensor(chosen[:, 0:B, :], onehot[:, 0, :, :], onehot[:, 1, :, :],
                                    ALU.add).then_inc(chosen_ok, 1)
            dve.wait_ge(ratio_ok, 1)
            then(nc.vector.tensor_scalar(total[:, :], ratio[:, :], 1.0, None, ALU.add))
            then(nc.vector.reciprocal(inverse[:, :], total[:, :]))
            then(nc.vector.tensor_scalar(weight[:, 0:B], inverse[:, :], gate[:, 1:2], None, ALU.mult))
            then(nc.vector.tensor_tensor(weight[:, B:2 * B], weight[:, 0:B], ratio[:, :], ALU.mult))
            dve.wait_ge(rank_made, 1)
            then(nc.vector.tensor_scalar(count_i[:, :], rank_ps[:, B * E:(B + 1) * E], float(ROWS - 1), None, ALU.add))
            then(nc.vector.tensor_scalar(tiles_i[:, :], count_i[:, :], 8, None, ALU.arith_shift_right))
            then(nc.vector.tensor_copy(tiles_f[:, :], tiles_i[:, :]))
            then(nc.vector.tensor_tensor_scan(ends[:, :], tiles_f[:, :], tiles_f[:, :], 0.0, ALU.add, ALU.bypass))
            then(nc.vector.tensor_tensor(starts[:, :], ends[:, :], tiles_f[:, :], ALU.subtract))
            then(nc.vector.tensor_tensor(
                tile_ge[:, :, :], cst[0:1, IOTA:IOTA + TCOLS].unsqueeze(2).to_broadcast([1, TCOLS, E]),
                ends[0:1, :].unsqueeze(1).to_broadcast([1, TCOLS, E]), ALU.is_ge))
            then(nc.vector.tensor_reduce(tile_exp[:, :], tile_ge[:, :, :], AX.X, ALU.add))
            nc.vector.tensor_scalar(tile_expert[:, :], tile_exp[:, :], float(E - 1), None,
                                    ALU.min).then_inc(experts_ok, 1)
            then(nc.vector.tensor_scalar(starts[:, :], starts[:, :], float(ROWS), None, ALU.mult))
            then(nc.vector.tensor_tensor(slot[:, :, :], rank_ps[:, 0:B * E].rearrange("p (b e) -> p b e", e=E),
                                         starts[:, :].unsqueeze(1).to_broadcast([P, B, E]), ALU.add))
            for choice in range(TOPK):
                then(nc.vector.tensor_tensor(slot_k[:, choice, :, :], onehot[:, choice, :, :], slot[:, :, :],
                                             ALU.mult))
            then(nc.vector.tensor_reduce(slots[:, :], slot_k[:, :, :, :].rearrange("p k b e -> p (k b) e"),
                                         AX.X, ALU.add))
            then(nc.vector.tensor_copy(slots_i[:, :], slots[:, :]))
            then(nc.vector.tensor_scalar(tile_i[:, :], slots_i[:, :], 7, None, ALU.arith_shift_right))
            then(nc.vector.tensor_copy(tile_f[:, :], tile_i[:, :]))
            then(nc.vector.scalar_tensor_tensor(out=lane_f[:, :], in0=tile_f[:, :], scalar=-float(P),
                                                in1=slots[:, :], op0=ALU.mult, op1=ALU.add))

            def hot(pair, seq, n):
                nc.vector.tensor_scalar(lane_hot[n][:, :], cst[:, IOTA:IOTA + P], lane_f[:, bass.ds(pair, 1)],
                                        None, ALU.is_equal).then_inc(hot_ok, 1)
                nc.vector.tensor_scalar(tile_hot[n][:, 0, :], cst[:, IOTA:IOTA + TCOLS],
                                        tile_f[:, bass.ds(pair, 1)], cst[:, bass.ds(TOKEN1 + seq, 1)],
                                        ALU.is_equal, ALU.mult).then_inc(hot_ok, 1)
                nc.vector.tensor_scalar(tile_hot[n][:, 1, :], cst[:, IOTA:IOTA + TCOLS],
                                        tile_f[:, bass.ds(pair, 1)], weight[:, bass.ds(pair, 1)],
                                        ALU.is_equal, ALU.mult).then_inc(hot_ok, 1)

            for n in range(HOT):
                hot(n, n, n)
            for choice in range(TOPK):
                with dve.Fori(0 if choice else 1, B // HOT) as i:
                    for n in range(HOT):
                        dve.wait_ge(hot_used, (choice * (B // HOT) + i - 1) * HOT + n + 1)
                        hot(choice * B + i * HOT + n, i * HOT + n, n)

            dve.wait_ge(hot_used, TOPK * B)
            then(nc.vector.tensor_copy(table[:, :, :], table_ps[:, 0:2 * TCOLS]))
            then(nc.vector.tensor_scalar(row_less1[:, :], table[:, 0, :], -1.0, None, ALU.add))
            then(nc.vector.tensor_scalar(empty[:, :], table[:, 0, :], 0.0, cst[:, SPARE1:SPARE1 + 1],
                                         ALU.is_equal, ALU.mult))
            nc.vector.tensor_scalar(gather_row[:, :], row_less1[:, :], 0.0, None, ALU.max).then_inc(slots_ok, 1)
            nc.vector.tensor_tensor(scatter_row[:, :], row_less1[:, :], empty[:, :], ALU.add).then_inc(slots_ok, 1)

            def rows_transposed(t, k, par):
                dve.wait_ge(rowsT_made, t + 1)
                nc.vector.tensor_copy(rowsT[par][:, :, :, :], t_ps[:, 0:4 * ROWS]).then_inc(rowsT_ok, 1)

            dve.wait_ge(b2_in, 16)
            dve.wait_ge(experts_ok, 1)
            rows_transposed(0, 0, 0)

            def split(t, par, pair):
                c = slice(2 * pair, 2 * pair + 2)
                piece = act32[:, 2 * pair * ROWS:2 * (pair + 1) * ROWS].rearrange("p (c n) -> p c n", c=2)
                dve.wait_ge(gelu_ok, 4 * t + pair + 1)
                nc.vector.tensor_copy(ghi[par][:, c, :], piece).then_inc(ghi_ok, 1)
                dve.wait_ge(ghi_ok, 4 * t + pair + 1)
                nc.vector.tensor_tensor(glo[par][:, c, :], piece, ghi[par][:, c, :],
                                        ALU.subtract).then_inc(glo_ok, 1)

            def weigh(t):
                e = dve.value_load(tile_expert[0:1, bass.ds(t, 1)], min_val=0, max_val=E - 1)
                if not is_first(t):
                    dve.wait_ge(yout_ok, 2 * t)
                dve.wait_ge(y_made, t + 1)
                for half in range(2):
                    nc.vector.tensor_tensor(ysum[half], y_ps[half][:, 0:D], b2bc[:, bass.ds(e * D, D)],
                                            ALU.add).then_inc(ysum_ok, 1)
                for half in range(2):
                    dve.wait_ge(ysum_ok, 2 * t + half + 1)
                    if not is_first(t):
                        dve.wait_ge(scattered[half], 16 * t)
                    nc.vector.tensor_scalar(yout[half], ysum[half], slot_gate[:, bass.ds(2 * t + half, 1)],
                                            None, ALU.mult).then_inc(yout_ok, 1)

            def tile(t, k, par):
                for pair in range(4):
                    split(t, par, pair)
                    if pair == 2 and not (isinstance(t, int) and t == TILES - 1):
                        rows_transposed(*following(t, k, par))
                if not is_first(t):
                    weigh(t - 1)

            over_tiles(dve, tile)
            weigh(TILES - 1)

        @block.tensor
        def _(pe):
            pe.wait_ge(const_in, 48)
            pe.wait_ge(halves_ok, 1)
            pe.wait_ge(pads_set, 1)
            identity_b = cstb[:, IDENT_B:IDENT_B + P]

            def transpose_kq(i, n):
                if real(i, n - 1):
                    pe.wait_ge(kqT_ok, num(i, n))
                pe.wait_ge(k_ok, num(i, n + 1))
                pe.wait_ge(q_ok, num(i, n + 1))
                for source, at in ((ksplit, 0), (qhi, 4)):
                    for g in range(4):
                        last = nc.tensor.transpose(kq_ps[:, (at + g) * P:(at + g + 1) * P],
                                                   source[:, 4 * g:4 * g + 4, :, :].rearrange("p h s d -> p (h s d)"),
                                                   identity_b)
                last.then_inc(kqT_made, 1)
                if real(i, n - 1):
                    pe.wait_ge(qlT_ok, num(i, n))
                for g in range(4):
                    last = nc.tensor.transpose(ql_ps[:, g * P:(g + 1) * P],
                                               qlo[:, 4 * g:4 * g + 4, :, :].rearrange("p h s d -> p (h s d)"),
                                               identity_b)
                last.then_inc(kqT_made, 1)

            def scores(i, n, which):
                t = num(i, n)
                pe.wait_ge(kqT_ok, t + 1)
                pe.wait_ge(qlT_ok, t + 1)
                for j in which:
                    rows = slice(32 * j, 32 * j + 32)
                    if real(i, n - 1):
                        if j == 0:
                            pe.wait_ge(outT_ok, t)
                        else:
                            pe.wait_ge(copied, 3 * t + j - 3)
                    for g in range(4):
                        to = sc_ps[j][:, g * P:(g + 1) * P]
                        nc.tensor.matmul(to, kqT[rows, 0, g, :], kqT[rows, 1, g, :], start=True, stop=False)
                        last = nc.tensor.matmul(to, kqT[rows, 0, g, :], kqT[rows, 2, g, :], start=False, stop=True)
                    last.then_inc(score_made, 1)

            def values(i, n):
                t = num(i, n)
                pe.wait_ge(s0_ok, t + 1)
                pe.wait_ge(selected, 3 * t + 3)
                for g in range(4):
                    for j in range(4):
                        h = 4 * g + j
                        last = nc.tensor.matmul(outT_ps[32 * j:32 * j + 32, g * P:(g + 1) * P],
                                                context[:, n % SLOTS, h * HD:h * HD + 32], smask[j][:, g, :],
                                                start=True, stop=True)
                last.then_inc(outT_made, 1)

            def transpose_outputs(i, n):
                pe.wait_ge(outT_ok, num(i, n + 1))
                if real(i, n - 1):
                    pe.wait_ge(x1_ok, num(i, n))
                for j in range(4):
                    last = nc.tensor.transpose(o_ps[:, j * P:(j + 1) * P], outT[:, j * P:(j + 1) * P],
                                               cst[:, IDENT:IDENT + P])
                last.then_inc(out_made, 1)

            def transpose_normed(i, n):
                pe.wait_ge(x2n_ok, num(i, n + 1))
                for d in range(DC):
                    last = nc.tensor.transpose(r_ps[:, d * P:(d + 1) * P], x2n[:, d * P:(d + 1) * P],
                                               cst[:, IDENT:IDENT + P])
                last.then_inc(x2T_made, 1)

            def router(i, n):
                pe.wait_ge(x2T_ok, num(i, n + 1))
                for d in range(DC):
                    last = nc.tensor.matmul(logit_ps, x2T[:, d, :], rw[:, d, :],
                                            start=(d == 0), stop=(d == DC - 1))
                last.then_inc(logit_made, 1)

            def step(i, n):
                if real(i, n):
                    scores(i, n, (1, 2, 3))
                if real(i, n - 1):
                    transpose_outputs(i, n - 1)
                if real(i, n):
                    scores(i, n, (0,))
                if real(i, n - 2):
                    transpose_normed(i, n - 2)
                if real(i, n + 1):
                    transpose_kq(i, n + 1)
                if real(i, n - 2):
                    router(i, n - 2)
                if real(i, n):
                    values(i, n)

            over_sequences(step)(pe)

            pe.wait_ge(chosen_ok, 2)
            for ahead in range(1, B + 1):
                nc.tensor.matmul(rank_ps[:, ahead * E:(B + 1) * E], cstb[:, ONES_B:ONES_B + P],
                                 chosen[:, 0:B + 1 - ahead, :].rearrange("p b e -> p (b e)"),
                                 start=(ahead == 1), stop=False, skip_group_check=True)
            last = nc.tensor.matmul(rank_ps[:, 0:(B + 1) * E], cstb[:, BEFORE_B:BEFORE_B + P],
                                    chosen[:, :, :].rearrange("p b e -> p (b e)"),
                                    start=False, stop=True, skip_group_check=True)
            last.then_inc(rank_made, 1)

            def invert(pair, n, first, last):
                pe.wait_ge(hot_ok, 3 * (pair + 1))
                nc.tensor.matmul(table_ps[:, 0:2 * TCOLS], lane_hot[n][:, :],
                                 tile_hot[n][:, :, :].rearrange("p a b -> p (a b)"),
                                 start=first, stop=last).then_inc(hot_used, 1)

            for n in range(HOT):
                invert(n, n, n == 0, False)
            with pe.Fori(1, TOPK * B // HOT - 1) as i:
                for n in range(HOT):
                    invert(i * HOT + n, n, False, False)
            for n in range(HOT):
                invert(TOPK * B - HOT + n, n, False, n == HOT - 1)

            def transpose_rows(t, k, par):
                pe.wait_ge(gathered[par], 32 * (k + 1))
                pe.wait_ge(rowsT_ok, t)
                for n in range(4):
                    for half in range(2):
                        at = n * ROWS + half * P
                        last = nc.tensor.transpose(t_ps[:, at:at + P], rows_in[par][:, half, n * P:(n + 1) * P],
                                                   identity_b)
                last.then_inc(rowsT_made, 1)

            def hidden(t, k, par, e):
                pe.wait_ge(rowsT_ok, t + 1)
                for c in range(HC):
                    if c % 2 == 0 and not is_first(t):
                        pe.wait_ge(gelu_ok, 4 * t - 3 + c // 2)
                    n = 0
                    for wpart, xpart in ((0, 0), (0, 1), (1, 0)):
                        for d in range(DC):
                            last = nc.tensor.matmul(
                                h_ps[c // 2][:, c % 2 * ROWS:(c % 2 + 1) * ROWS],
                                w1s[:, bass.ds(e * (2 * DC * H) + (wpart * DC + d) * H + c * P, P)],
                                rowsT[par][:, xpart, d, :], start=(n == 0), stop=(n == 3 * DC - 1))
                            n += 1
                    if c % 2 == 1:
                        last.then_inc(h_made, 1)

            def output(t, k, par, e):
                if not is_first(t):
                    pe.wait_ge(ysum_ok, 2 * t)
                for c in range(HC):
                    if c % 2 == 0:
                        pe.wait_ge(glo_ok, 4 * t + c // 2 + 1)
                    for half in range(2):
                        rows = slice(half * P, (half + 1) * P)
                        for gpart, wpart in ((ghi, 0), (glo, 0), (ghi, 1)):
                            last = nc.tensor.matmul(
                                y_ps[half][:, 0:D], gpart[par][:, c, rows],
                                w2s[:, bass.ds(e * (2 * HC * D) + (wpart * HC + c) * D, D)],
                                start=(c == 0 and wpart == 0 and gpart is ghi), stop=(c == HC - 1 and wpart == 1))
                last.then_inc(y_made, 1)

            pe.wait_ge(experts_ok, 1)
            pe.wait_ge(w1lo_ok, B)
            pe.wait_ge(w2lo_ok, B)
            transpose_rows(0, 0, 0)

            def expert(t):
                return pe.value_load(tile_expert[0:1, bass.ds(t, 1)], min_val=0, max_val=E - 1)

            hidden(0, 0, 0, expert(0))
            transpose_rows(1, 0, 1)

            def tile(t, k, par):
                if not (isinstance(t, int) and t == TILES - 1):
                    hidden(*following(t, k, par), expert(t + 1))
                if not (isinstance(t, int) and t >= TILES - 2):
                    transpose_rows(t + 2, k + 1, par)
                output(t, k, par, expert(t))

            over_tiles(pe, tile)


def kernel(x, ctx_1024, g_xattn, g_ffn, L0_ffn_router_w, L0_ffn_w1, L0_ffn_b1, L0_ffn_w2, L0_ffn_b2):
    import concourse.bacc as bacc
    from concourse.bass_utils import run_bass_kernel_spmd

    const, const_b = constants()
    arrays = {
        "x_in": np.ascontiguousarray(x),
        "ctx_in": np.ascontiguousarray(ctx_1024),
        "gates_in_": np.concatenate([np.asarray(g_xattn), np.asarray(g_ffn)]).reshape(1, 2),
        "router_in": np.ascontiguousarray(L0_ffn_router_w),
        "w1_in": np.ascontiguousarray(L0_ffn_w1),
        "b1_in": np.ascontiguousarray(np.asarray(L0_ffn_b1).reshape(E * HC, P).T),
        "w2_in": np.ascontiguousarray(L0_ffn_w2),
        "b2_in_": np.ascontiguousarray(np.asarray(L0_ffn_b2).reshape(1, E * D)),
        "const_in_": const,
        "const_b_in_": const_b,
    }
    nc = bacc.Bacc("TRN2", target_bir_lowering=False, num_devices=1)
    args = [nc.dram_tensor(n, a.shape, mybir.dt.from_np(a.dtype), kind="ExternalInput").ap() for n, a in arrays.items()]
    out = nc.dram_tensor("out_rows", [TOKENS + SPARE, D], F32, kind="ExternalOutput").ap()
    build(nc, *args, out)
    result = run_bass_kernel_spmd(nc, [arrays], core_ids=[0])
    return result.results[0]["out_rows"][:TOKENS].reshape(B, S, D)
```

```python
import math
from contextlib import ExitStack

import numpy as np

import concourse.bass as bass
from concourse import mybir

ALU = mybir.AluOpType
ACT = mybir.ActivationFunctionType
AX = mybir.AxisListType
F32 = mybir.dt.float32
BF16 = mybir.dt.bfloat16
I32 = mybir.dt.int32
U32 = mybir.dt.uint32

P = 128
B, S, D = 16, 128, 256
HEADS, HD = 16, 16
E, H, TOPK = 8, 1024, 2
TOKENS = B * S
DC = D // P
HC = H // P
UNITS = TOKENS * TOPK // P + E - 1
PAIRS = (UNITS - E) // 2
SINGLES = max(E, UNITS - 2 * PAIRS)
TILES = PAIRS + SINGLES
UNITS_RUN = 2 * PAIRS + SINGLES
TCOLS = UNITS_RUN + UNITS_RUN % 2
ROWS = 2 * P
EPS = 1e-5
SLOTS = 4
HOT = 8
HOTS = TOPK * B // HOT
SPARE = P

CQ, SQ, CK, SK = 0, D, 2 * D, 3 * D
IDENT = 4 * D
CAUSAL = IDENT + P
IOTA = CAUSAL + P
TOKEN1 = IOTA + P
SPARE1 = TOKEN1 + B
BELOW8 = SPARE1 + 1
NCONST = BELOW8 + E
IDENT_B, BEFORE_B, ONES_B, NCONST_B = 0, P, 2 * P, 3 * P


def constants():
    half = HD // 2
    base = (np.arange(0, HD, 2, dtype=np.float32) + np.float32(0.4 * HD)) / np.float32(1.4 * HD)
    pos = np.arange(S, dtype=np.float64)
    scale = base.astype(np.float64)[None, :] ** (pos / 512.0)[:, None]
    freq = (1.0 / 10000.0 ** (np.arange(half, dtype=np.float32) / np.float32(half))).astype(np.float32)
    angle = (pos[:, None].astype(np.float32) * freq[None, :]).astype(np.float64)
    gamma = (1.0 - np.exp(np.linspace(math.log(1 / 32), math.log(1 / 512), HEADS))).astype(np.float32)
    decay = gamma.astype(np.float64)[None, :] ** pos[:, None]
    c = np.zeros((P, NCONST), np.float32)
    for at_cos, at_sin, factor in ((CQ, SQ, decay[:, :, None] * scale[:, None, :]),
                                   (CK, SK, 1 / (decay[:, :, None] * scale[:, None, :]))):
        cos = np.cos(angle)[:, None, :] * factor
        sin = np.sin(angle)[:, None, :] * factor
        c[:, at_cos:at_cos + D] = np.stack([cos, cos], -1).reshape(S, D)
        c[:, at_sin:at_sin + D] = np.stack([-sin, sin], -1).reshape(S, D)
    c[:, IDENT:IDENT + P] = np.eye(P)
    c[:, CAUSAL:CAUSAL + P] = np.triu(np.ones((P, P)))
    c[:, IOTA:IOTA + P] = np.arange(P)
    c[:, TOKEN1:TOKEN1 + B] = 1 + np.arange(P)[:, None] + P * np.arange(B)
    c[:, SPARE1] = 1 + TOKENS + np.arange(P)
    c[:, BELOW8:BELOW8 + E] = np.arange(E) - E
    cb = np.zeros((P, NCONST_B), np.float32)
    cb[:, IDENT_B:IDENT_B + P] = np.eye(P)
    cb[:, BEFORE_B:BEFORE_B + P] = np.triu(np.ones((P, P)), 1)
    cb[:, ONES_B:ONES_B + P] = 1
    return c, cb


def swapped(ap):
    return ap.rearrange("p (a b) -> p a b", b=2)[:, :, ::-1]


def pairs(ap):
    return ap.rearrange("p (a b) -> p a b", b=2)


def build(nc, x, ctx, gates, router_w, w1, b1, w2, b2, const, const_b, out):
    with ExitStack() as stack:
        def sb(name, shape, dt):
            return stack.enter_context(nc.sbuf_tensor(name, shape, dt))

        def psum(name, shape, dt=F32):
            return stack.enter_context(nc.psum_tensor(name, shape, dt))

        def sem(name):
            return stack.enter_context(nc.semaphore(name))

        def sem2(name):
            return [sem(f"{name}{par}") for par in range(2)]

        x_rows = x.rearrange("b s d -> (b s) d")
        ctx_rows = ctx.rearrange("b s d -> (b s) d")
        w1_rows = w1.rearrange("e d h -> (e d) h")
        w2_rows = w2.rearrange("e h d -> (e h) d")
        normed_dram = nc.dram_tensor("normed_rows", [TOKENS, 2 * D], BF16, kind="Internal").ap()

        cst = sb("cst", [P, NCONST], F32)
        cstb = sb("cstb", [P, NCONST_B], BF16)
        gate = sb("gate", [P, 2], F32)
        minus_half = sb("minus_half", [P, 2], F32)
        rw = sb("rw", [P, DC, E], F32)
        b1c = sb("b1c", [P, E * HC], F32)
        zero_rows = sb("zero_rows", [P, D], F32)
        w1s = sb("w1s", [P, E * 2 * DC * H], BF16)
        w2s = sb("w2s", [P, E * 2 * HC * D], BF16)
        raw = sb("raw", [P, 4 * H], F32)
        raw1 = [raw[:, par * H:(par + 1) * H] for par in range(2)]
        raw2 = [raw[:, (2 + par) * H:(3 + par) * H] for par in range(2)]
        b2bc = raw[:, 0:E * D]
        act32 = raw[:, E * D:E * D + HC * ROWS]

        seq_in = sb("seq_in", [P, SLOTS * D], F32)
        context = sb("context", [P, SLOTS, D + HD], F32)
        xin = [seq_in[:, s * D:(s + 1) * D] for s in range(SLOTS)]
        cin = [context[:, s, 0:D] for s in range(SLOTS)]
        stats = sb("stats", [P, 6], F32)
        moments = sb("moments", [P, 2, 2], F32)
        mean1, mean2 = moments[:, 0, :], moments[:, 1, :]
        veps = sb("veps", [P, 2], F32)
        rstd = sb("rstd", [P, 2], F32)
        rotary = sb("rotary", [P, 5 * D], F32)
        xn, turn, kturn, qrot, krot = (rotary[:, n * D:(n + 1) * D] for n in range(5))
        ksplit = sb("ksplit", [P, HEADS, 2, HD], BF16)
        qhi = sb("qhi", [P, HEADS, 2, HD], BF16)
        qlo = sb("qlo", [P, HEADS, 2, HD], BF16)
        kqT = sb("kqT", [P, 3, 4, P], BF16)
        masked = sb("masked", [P, 4 * 4 * P], F32)
        smask = [masked[:, 4 * j * P:4 * (j + 1) * P].rearrange("p (g n) -> p g n", g=4) for j in range(4)]
        halves = masked[:, 0:NCONST_B]
        stats2 = sb("stats2", [P, 6], F32)
        x2n = sb("x2n", [P, D], F32)
        x2split = [sb(f"x2split{s}", [P, 2 * D], BF16) for s in range(SLOTS)]
        x2T = sb("x2T", [P, DC, P], F32)
        outT = sb("outT", [P, 4 * P], F32)

        logits = sb("logits", [P, B * E], F32)
        others = sb("others", [P, B * E], F32)
        ties = sb("ties", [P, B * E], F32)
        first = sb("first", [P, B], F32)
        best = sb("best", [P, TOPK, B], F32)
        onehot = sb("onehot", [P, TOPK, B, E], F32)
        chosen = sb("chosen", [P, B + 1, E], BF16)
        count_i = sb("count_i", [P, E], I32)
        parts_i = sb("parts_i", [P, 2, E], I32)
        parts_f = sb("parts_f", [P, 2, E], F32)
        units, twos = parts_f[:, 0, :], parts_f[:, 1, :]
        pair_end = sb("pair_end", [P, E], F32)
        pair_start = sb("pair_start", [P, E], F32)
        paired = sb("paired", [P, E], F32)
        single = sb("single", [P, E], F32)
        single_end = sb("single_end", [P, E], F32)
        single_start = sb("single_start", [P, E], F32)
        wide_base = sb("wide_base", [P, E], F32)
        wide_rows = sb("wide_rows", [P, E], F32)
        jump = sb("jump", [P, E], F32)
        slot = sb("slot", [P, B, E], F32)
        beyond = sb("beyond", [P, B, E], F32)
        slot_k = sb("slot_k", [P, TOPK, B, E], F32)
        slots = sb("slots", [P, TOPK * B], F32)
        slots_i = sb("slots_i", [P, TOPK * B], I32)
        tile_i = sb("tile_i", [P, TOPK * B], I32)
        tile_f = sb("tile_f", [P, TOPK * B], F32)
        lane_f = sb("lane_f", [P, TOPK * B], F32)
        gap = sb("gap", [P, B], F32)
        ratio = sb("ratio", [P, B], F32)
        total = sb("total", [P, B], F32)
        inverse = sb("inverse", [P, B], F32)
        weight = sb("weight", [P, TOPK * B], F32)
        table = sb("table", [P, 2, TCOLS], F32)
        slot_gate = table[:, 1, :]
        row_less1 = sb("row_less1", [P, TCOLS], F32)
        empty = sb("empty", [P, TCOLS], F32)
        gather_row = sb("gather_row", [P, TCOLS], I32)
        scatter_row = sb("scatter_row", [P, TCOLS], I32)
        gather_now = [[sb(f"gather_now{p}{half}", [P, 1], I32) for half in range(2)] for p in range(2)]
        scatter_now = [sb(f"scatter_now{half}", [P, 1], I32) for half in range(2)]
        tile_ge = sb("tile_ge", [1, TILES, E], F32)
        tile_exp = sb("tile_exp", [1, TILES], F32)
        tile_expert = sb("tile_expert", [1, TILES], I32)

        rows_in = [seq_in[:, 2 * p * D:2 * (p + 1) * D].bitcast(BF16).rearrange("p (h d) -> p h d", h=2)
                   for p in range(2)]
        rowsT = [rotary[:, 2 * p * D:2 * (p + 1) * D].bitcast(BF16).rearrange("p (s c n) -> p s c n", s=2, c=DC)
                 for p in range(2)]
        gelu_even = sb("gelu_even", [P, 2, HC, ROWS], BF16)
        gelu_odd = masked[:, :].bitcast(BF16).rearrange("p (s c n) -> p s c n", s=2, c=HC)
        ghi = [gelu_even[:, 0, :, :], gelu_odd[:, 0, :, :]]
        glo = [gelu_even[:, 1, :, :], gelu_odd[:, 1, :, :]]
        lane_hot = [raw[:, c * HOT * P:(c + 1) * HOT * P].rearrange("p (n l) -> p n l", n=HOT) for c in range(HOTS)]
        room = [masked[:, :], gelu_even[:, :, :, :].rearrange("p s c n -> p (s c n)").bitcast(F32)]
        width = HOT * TCOLS
        tile_hot = [room[c % 2][:, c // 2 * 2 * width:(c // 2 + 1) * 2 * width].rearrange("p (n a l) -> p n a l",
                                                                                          n=HOT, a=2)
                    for c in range(HOTS)]
        tile_eq = [room[c][:, 4 * width:5 * width].rearrange("p (n l) -> p n l", n=HOT) for c in range(2)]
        ysum = [cin[half] for half in range(2)]
        yout = [cin[2 + half] for half in range(2)]

        bank = [psum(f"bank{n}", [P, 512]) for n in range(8)]
        sc_ps = bank[0:4]
        kq_ps = bank[4][:, :].bitcast(BF16)
        ql_ps = bank[5][:, :].bitcast(BF16)
        outT_ps = bank[0]
        o_ps = bank[6]
        r_ps = bank[7]
        logit_ps = r_ps[:, D:D + E]
        rank_ps = bank[0]
        table_ps = bank[1]
        h_ps = bank[0:4]
        t_ps = bank[4][:, :].bitcast(BF16)
        y_ps = [bank[5], bank[6]]

        const_in, gates_in, b2_in = sem("const_in"), sem("gates_in"), sem("b2_in")
        zeros_set, zeros_out = sem("zeros_set"), sem("zeros_out")
        half_set, gates_ready, halves_ok = sem("half_set"), sem("gates_ready"), sem("halves_ok")
        halves_in = sem("halves_in")
        xc_in, raw_in = [sem(f"xc_in{s}") for s in range(SLOTS)], sem2("raw_in")
        stats1_ok, mean1_ok, stats2_ok, mean2_ok = sem("stats1_ok"), sem("mean1_ok"), sem("stats2_ok"), sem("mean2_ok")
        veps_ok, rstd_ok = sem("veps_ok"), sem("rstd_ok")
        kterms, krot_ok, khi_ok, k_ok = sem("kterms"), sem("krot_ok"), sem("khi_ok"), sem("k_ok")
        xn_ok, qterms, qrot_ok, qhi_ok, q_ok = sem("xn_ok"), sem("qterms"), sem("qrot_ok"), sem("qhi_ok"), sem("q_ok")
        kqT_made, kqT_ok, qlT_ok = sem("kqT_made"), sem("kqT_ok"), sem("qlT_ok")
        score_made = sem("score_made")
        s0_ok, copied, selected = sem("s0_ok"), sem("copied"), sem("selected")
        pads_set, outT_made, outT_ok, out_made = sem("pads_set"), sem("outT_made"), sem("outT_ok"), sem("out_made")
        x1_ok = sem("x1_ok")
        x1_out, x2_out = sem2("x1_out"), sem2("x2_out")
        x2n_ok, x2hi_ok, x2lo_ok = sem("x2n_ok"), sem("x2hi_ok"), sem("x2lo_ok")
        x2T_made, x2T_ok, logit_made, logit_ok = sem("x2T_made"), sem("x2T_ok"), sem("logit_made"), sem("logit_ok")
        w1hi_ok, w1lo_ok, w2hi_ok, w2lo_ok = sem("w1hi_ok"), sem("w1lo_ok"), sem("w2hi_ok"), sem("w2lo_ok")
        route_step, chosen_ok, rank_made = sem("route_step"), sem("chosen_ok"), sem("rank_made")
        gap_ok, ratio_ok = sem("gap_ok"), sem("ratio_ok")
        lanes_ok, lane_hot_ok, tile_eq_ok = sem("lanes_ok"), sem("lane_hot_ok"), sem("tile_eq_ok")
        token_hot_ok, weight_hot_ok, hot_used = sem("token_hot_ok"), sem("weight_hot_ok"), sem("hot_used")
        experts_ok, slots_ok = sem("experts_ok"), sem("slots_ok")
        gathered, scattered = sem2("gathered"), sem2("scattered")
        gather_set, scatter_set = sem("gather_set"), sem("scatter_set")
        rowsT_made, rowsT_ok = sem("rowsT_made"), sem("rowsT_ok")
        h_made, gelu_ok, ghi_ok, glo_ok = sem("h_made"), sem("gelu_ok"), sem("ghi_ok"), sem("glo_ok")
        y_made, ysum_ok, yout_ok = sem("y_made"), sem("ysum_ok"), sem("yout_ok")

        block = stack.enter_context(nc.Block())

        def over_sequences(step):
            def run(eng):
                for n in range(-2, 2):
                    step(0, n)
                with eng.Fori(0, B // SLOTS - 1) as i:
                    for n in range(2, 2 + SLOTS):
                        step(i, n)
                for n in range(B - 2, B + 2):
                    step(0, n)
            return run

        def real(i, n):
            return not isinstance(i, int) or 0 <= n < B

        def num(i, n):
            return SLOTS * i + n

        def half_num(i, n):
            return SLOTS // 2 * i + n // 2

        def w1_at(i, n):
            return half_num(i, n) * (2 * DC * H) + n % 2 * H

        def w2_at(i, n):
            return half_num(i, n) * (2 * HC * D) + n % 2 * H

        def own(eng, sem, value):
            if not isinstance(value, int):
                value = eng.lower_val(value)
            eng.wait_ge(const_in, 48)
            eng.wait_ge(sem, value)

        def shift(tile, by):
            t, k, par, one = tile
            return t + by, k + (par + by) // 2, (par + by) % 2, (t + by >= PAIRS if isinstance(t, int) else one)

        def tile_exists(tile):
            return not isinstance(tile[0], int) or 0 <= tile[0] < TILES

        def parts(tile):
            t, k, par, one = tile
            if one:
                return [(t + PAIRS, (par + PAIRS) % 2, k + (par + PAIRS) // 2)]
            return [(2 * t, 0, t), (2 * t + 1, 1, t)]

        def units_through(tile):
            return parts(tile)[-1][0] + 1

        def units_of_parity_through(tile):
            t, k, par, one = tile
            return k + 1 + (PAIRS + 1 - par) // 2 if one else 2 * (k + 1)

        def over_tiles(eng, step):
            def peeled(first, last):
                for t in range(first, last):
                    step((t, t // 2, t % 2, t >= PAIRS))

            def looped(first, last, one):
                with eng.Fori(first // 2, last // 2) as i:
                    step((2 * i, i, 0, one))
                    step((2 * i + 1, i, 1, one))

            wide_last = (PAIRS - 3) // 2 * 2
            single_first = (PAIRS + 2) // 2 * 2
            single_last = (TILES - 3) // 2 * 2
            peeled(0, 2)
            looped(2, wide_last, False)
            peeled(wide_last, single_first)
            looped(single_first, single_last, True)
            peeled(single_last, TILES)

        @block.sync
        def _(sp):
            def load_seq(i, n):
                rows = bass.ds(num(i, n) * P, P)
                sp.dma_start(xin[n % SLOTS], x_rows[rows, :]).then_inc(xc_in[n % SLOTS], 16)
                sp.dma_start(cin[n % SLOTS], ctx_rows[rows, :]).then_inc(xc_in[n % SLOTS], 16)

            def load_raw(i, n):
                sp.dma_start(raw1[n % 2], w1_rows[bass.ds(num(i, n) * P, P), :]).then_inc(raw_in[n % 2], 16)
                sp.dma_start(raw2[n % 2].rearrange("p (c d) -> p c d", c=4),
                             w2_rows[bass.ds(num(i, n) * 4 * P, 4 * P), :].rearrange("(c p) d -> p c d", p=P)
                             ).then_inc(raw_in[n % 2], 16)

            load_seq(0, 0)
            sp.dma_start(cst[:, :], const).then_inc(const_in, 16)
            sp.dma_start(halves[:, :], const_b).then_inc(halves_in, 16)
            sp.dma_start(gate[:, :], gates.to_broadcast([P, 2])).then_inc(gates_in, 16)
            sp.dma_start(rw[:, :, :], router_w.rearrange("(c p) e -> p c e", p=P)).then_inc(const_in, 16)
            sp.dma_start(b1c[:, :], b1).then_inc(const_in, 16)
            load_seq(0, 1)
            load_raw(0, 0)
            load_seq(0, 2)
            load_raw(0, 1)
            load_seq(0, 3)
            sp.wait_ge(zeros_set, 1)
            sp.dma_start(out[TOKENS:TOKENS + SPARE, :], zero_rows[:, :]).then_inc(zeros_out, 16)

            def step(i, n):
                if real(i, n - 2):
                    if real(i, n + 2):
                        sp.wait_ge(x2n_ok, num(i, n - 1))
                        sp.wait_ge(x1_out[n % 2], 16 * half_num(i, n))
                        load_seq(i, n + 2)
                    sp.wait_ge(x2lo_ok, num(i, n - 1))
                    sp.dma_start(normed_dram[bass.ds(num(i, n - 2) * P, P), :],
                                 x2split[(n - 2) % SLOTS][:, :]).then_inc(x2_out[n % 2], 16)
                if real(i, n - 1):
                    sp.wait_ge(x1_ok, num(i, n))
                    sp.dma_start(out[bass.ds(num(i, n - 1) * P, P), :],
                                 xin[(n - 1) % SLOTS]).then_inc(x1_out[(n - 1) % 2], 16)
                    if real(i, n + 1):
                        if real(i, n - 2):
                            sp.wait_ge(x2_out[n % 2], 16 * half_num(i, n))
                        sp.wait_ge(w1lo_ok, num(i, n))
                        sp.wait_ge(w2lo_ok, num(i, n))
                        load_raw(i, n + 1)

            over_sequences(step)(sp)
            sp.wait_ge(hot_used, HOTS // 2)
            sp.dma_start(b2bc, b2.to_broadcast([P, E * D])).then_inc(b2_in, 16)
            sp.wait_ge(scattered[0], 16 * ((UNITS_RUN + 1) // 2))
            sp.wait_ge(scattered[1], 16 * (UNITS_RUN // 2))

        @block.gpsimd
        def _(pool):
            pool.memset(zero_rows[:, :], 0.0).then_inc(zeros_set, 1)
            pool.memset(context[:, :, D:D + HD], 0.0).then_inc(pads_set, 1)
            pool.memset(minus_half[:, :], -0.5).then_inc(half_set, 1)
            pool.wait_ge(half_set, 1)

            def inverse_roots(i, n):
                one, two = real(i, n + 2), real(i, n - 1)
                columns = slice(0 if one else 1, 2 if two else 1)
                if one:
                    own(pool, mean1_ok, num(i, n + 3))
                if two:
                    own(pool, mean2_ok, num(i, n))
                pool.tensor_scalar(veps[:, columns], moments[:, columns, 1], EPS, None, ALU.add).then_inc(veps_ok, 1)
                pool.wait_ge(veps_ok, num(i, n + 3))
                pool.tensor_tensor(rstd[:, columns], veps[:, columns], minus_half[:, columns],
                                   ALU.pow).then_inc(rstd_ok, 1)

            def select(i, n, j):
                own(pool, copied, 3 * num(i, n) + j)
                pool.affine_select(out=smask[j], in_=smask[j], compare_op=ALU.is_ge, fill=0.0, base=0,
                                   pattern=[[0, 4], [1, P]], channel_multiplier=-1).then_inc(selected, 1)

            def step(i, n):
                if real(i, n):
                    select(i, n, 1)
                    select(i, n, 2)
                if real(i, n + 2) or real(i, n - 1):
                    inverse_roots(i, n)
                if real(i, n):
                    select(i, n, 3)
                    pool.wait_ge(w2hi_ok, num(i, n + 1))
                    at = w2_at(i, n)
                    pool.tensor_tensor(w2s[:, bass.ds(at + HC * D, H)], raw2[n % 2], w2s[:, bass.ds(at, H)],
                                       ALU.subtract).then_inc(w2lo_ok, 1)

            over_sequences(step)(pool)

            def gather(tile):
                par = tile[2]
                for half, (unit, _, _) in enumerate(parts(tile)):
                    pool.tensor_copy(gather_now[par][half][:, :],
                                     gather_row[:, bass.ds(unit, 1)]).then_inc(gather_set, 1)
                    own(pool, gather_set, unit + 1)
                    pool.indirect_dma_start(
                        out=rows_in[par][:, half, :], out_offset=None, in_=normed_dram,
                        in_offset=bass.IndirectOffsetOnAxis(ap=gather_now[par][half][:, :], axis=0),
                        bounds_check=TOKENS - 1).then_inc(gathered[par], 16)

            for c in range(HOTS):
                pool.wait_ge(tile_eq_ok, c + 1)
                pool.tensor_tensor(tile_hot[c][:, :, 1, :], tile_eq[c % 2],
                                   weight[:, c * HOT:(c + 1) * HOT].unsqueeze(2).to_broadcast([P, HOT, TCOLS]),
                                   ALU.mult).then_inc(weight_hot_ok, 1)
            pool.wait_ge(slots_ok, 2)
            for par in range(2):
                pool.wait_ge(x2_out[par], 16 * (B // 2))
                pool.wait_ge(x1_out[par], 16 * (B // 2))
            pool.wait_ge(zeros_out, 16)
            start = (0, 0, 0, False)
            gather(start)
            gather(shift(start, 1))
            pool.wait_ge(rowsT_made, 1)
            gather(shift(start, 2))

            def step_c(tile):
                if tile_exists(shift(tile, 3)):
                    pool.wait_ge(rowsT_made, tile[0] + 2)
                    gather(shift(tile, 3))
                for unit, side, k in parts(tile):
                    pool.tensor_copy(scatter_now[side][:, :],
                                     scatter_row[:, bass.ds(unit, 1)]).then_inc(scatter_set, 1)
                    own(pool, scatter_set, unit + 1)
                    pool.wait_ge(yout_ok, unit + 1)
                    own(pool, scattered[1 - side], 16 * (k + side))
                    pool.indirect_dma_start(
                        out=out, out_offset=bass.IndirectOffsetOnAxis(ap=scatter_now[side][:, :], axis=0),
                        in_=yout[side], in_offset=None, bounds_check=TOKENS + SPARE - 1,
                        compute_op=ALU.add).then_inc(scattered[side], 16)

            over_tiles(pool, step_c)

        @block.scalar
        def _(act):
            act.wait_ge(gates_in, 16)
            nc.scalar.activation(gate[:, :], gate[:, :], ACT.Tanh).then_inc(gates_ready, 1)
            act.wait_ge(halves_in, 16)
            nc.scalar.copy(cstb[:, :], halves[:, :]).then_inc(halves_ok, 1)

            def heads(ap):
                return ap.rearrange("p (h d) -> p h d", d=HD)

            def step(i, n):
                if real(i, n - 1):
                    act.wait_ge(outT_made, num(i, n))
                    if real(i, n - 2):
                        act.wait_ge(out_made, num(i, n - 1))
                    nc.scalar.copy(outT[:, :], outT_ps[:, :]).then_inc(outT_ok, 1)
                if real(i, n):
                    for j in range(1, 4):
                        act.wait_ge(score_made, 4 * num(i, n) + j)
                        nc.scalar.copy(smask[j], sc_ps[j][:, :]).then_inc(copied, 1)
                if real(i, n - 2):
                    act.wait_ge(x2T_made, num(i, n - 1))
                    nc.scalar.copy(x2T[:, :, :], r_ps[:, 0:D]).then_inc(x2T_ok, 1)
                if real(i, n + 1):
                    act.wait_ge(kqT_made, 2 * num(i, n + 1) + 1)
                    nc.scalar.copy(kqT[:, 0:2, :, :], kq_ps[:, 0:8 * P]).then_inc(kqT_ok, 1)
                    act.wait_ge(kqT_made, 2 * num(i, n + 2))
                    nc.scalar.copy(kqT[:, 2, :, :], ql_ps[:, 0:4 * P]).then_inc(qlT_ok, 1)
                if real(i, n):
                    act.wait_ge(raw_in[n % 2], 32 * (half_num(i, n) + 1))
                    nc.scalar.copy(w2s[:, bass.ds(w2_at(i, n), H)], raw2[n % 2]).then_inc(w2hi_ok, 1)
                if real(i, n + 2):
                    act.wait_ge(krot_ok, num(i, n + 3))
                    nc.scalar.copy(ksplit[:, :, 0, :], heads(krot)).then_inc(khi_ok, 1)
                if real(i, n):
                    nc.scalar.copy(w1s[:, bass.ds(w1_at(i, n), H)], raw1[n % 2]).then_inc(w1hi_ok, 1)
                if real(i, n - 1):
                    act.wait_ge(x2n_ok, num(i, n))
                    nc.scalar.copy(x2split[(n - 1) % SLOTS][:, 0:D], x2n[:, :]).then_inc(x2hi_ok, 1)
                if real(i, n + 2):
                    act.wait_ge(qrot_ok, num(i, n + 3))
                    nc.scalar.copy(qhi[:, :, :, :],
                                   heads(qrot).unsqueeze(2).to_broadcast([P, HEADS, 2, HD])).then_inc(qhi_ok, 1)

            over_sequences(step)(act)

            act.wait_ge(gap_ok, 1)
            nc.scalar.activation(ratio[:, :], gap[:, :], ACT.Exp).then_inc(ratio_ok, 1)

            act.wait_ge(experts_ok, 1)
            act.wait_ge(w1lo_ok, B)
            act.wait_ge(w2lo_ok, B)

            def step_c(tile):
                t, one = tile[0], tile[3]
                n = P if one else ROWS
                e = act.value_load(tile_expert[0:1, bass.ds(t, 1)], min_val=0, max_val=E - 1)
                for pair in range(4):
                    act.wait_ge(h_made, 4 * t + pair + 1)
                    if tile_exists(shift(tile, -1)):
                        act.wait_ge(glo_ok, 4 * t + pair - 3)
                    for c in (2 * pair, 2 * pair + 1):
                        last = nc.scalar.activation(act32[:, c * ROWS:c * ROWS + n],
                                                    h_ps[pair][:, c % 2 * ROWS:c % 2 * ROWS + n],
                                                    ACT.Gelu, bias=b1c[:, bass.ds(e * HC + c, 1)])
                    last.then_inc(gelu_ok, 1)

            over_tiles(act, step_c)

        @block.vector
        def _(dve):
            dve.wait_ge(const_in, 48)
            dve.wait_ge(gates_ready, 1)

            def statistics(count, data, stat, stat_ok, mean, mean_ok):
                nc.vector.bn_stats(stat[:, :], data).then_inc(stat_ok, 1)
                own(dve, stat_ok, count)
                nc.vector.bn_aggr(mean, stat[:, :]).then_inc(mean_ok, 1)

            def heads(ap):
                return ap.rearrange("p (h d) -> p h d", d=HD)

            def prepare_k(i, n):
                s = n % SLOTS
                nc.vector.tensor_tensor(krot, cin[s], cst[:, CK:CK + D], ALU.mult).then_inc(kterms, 1)
                nc.vector.tensor_tensor(pairs(kturn), swapped(cin[s]), pairs(cst[:, SK:SK + D]),
                                        ALU.mult).then_inc(kterms, 1)
                dve.wait_ge(kterms, 2 * num(i, n + 1))
                nc.vector.tensor_tensor(krot, krot, kturn, ALU.add).then_inc(krot_ok, 1)

            def prepare_q(i, n):
                s = n % SLOTS
                dve.wait_ge(rstd_ok, num(i, n + 1))
                nc.vector.tensor_scalar(xn, xin[s], mean1[:, 0:1], rstd[:, 0:1],
                                        ALU.subtract, ALU.mult).then_inc(xn_ok, 1)
                dve.wait_ge(xn_ok, num(i, n + 1))
                nc.vector.tensor_tensor(qrot, xn, cst[:, CQ:CQ + D], ALU.mult).then_inc(qterms, 1)
                nc.vector.tensor_tensor(pairs(turn), swapped(xn), pairs(cst[:, SQ:SQ + D]),
                                        ALU.mult).then_inc(qterms, 1)
                dve.wait_ge(qterms, 2 * num(i, n + 1))
                nc.vector.tensor_tensor(qrot, qrot, turn, ALU.add).then_inc(qrot_ok, 1)

            def split_kq(i, n):
                dve.wait_ge(khi_ok, num(i, n + 1))
                nc.vector.tensor_tensor(ksplit[:, :, 1, :], heads(krot), ksplit[:, :, 0, :],
                                        ALU.subtract).then_inc(k_ok, 1)
                dve.wait_ge(qhi_ok, num(i, n + 1))
                nc.vector.tensor_tensor(qlo[:, :, :, :], heads(qrot).unsqueeze(2).to_broadcast([P, HEADS, 2, HD]),
                                        qhi[:, :, :, :], ALU.subtract).then_inc(q_ok, 1)

            def step(i, n):
                last = (n - 1) % SLOTS
                if real(i, n + 2):
                    s = (n + 2) % SLOTS
                    dve.wait_ge(xc_in[s], 32 * (i + (n + 2) // SLOTS + 1))
                    statistics(num(i, n + 3), xin[s], stats, stats1_ok, mean1, mean1_ok)
                    prepare_k(i, n + 2)
                if real(i, n - 1):
                    dve.wait_ge(out_made, num(i, n))
                    by_head = xin[last].rearrange("p (h d) -> p h d", d=HD)
                    nc.vector.scalar_tensor_tensor(
                        out=by_head, in0=o_ps[:, :].rearrange("p (h d) -> p h d", d=32)[:, :, 0:HD],
                        scalar=gate[:, 0:1], in1=by_head, op0=ALU.mult, op1=ALU.add).then_inc(x1_ok, 1)
                    dve.wait_ge(x1_ok, num(i, n))
                    statistics(num(i, n), xin[last], stats2, stats2_ok, mean2, mean2_ok)
                if real(i, n):
                    dve.wait_ge(score_made, 4 * num(i, n) + 4)
                    nc.vector.tensor_tensor(smask[0], sc_ps[0][:, :].rearrange("p (g n) -> p g n", g=4),
                                            cst[:, CAUSAL:CAUSAL + P].unsqueeze(1).to_broadcast([P, 4, P]),
                                            ALU.mult).then_inc(s0_ok, 1)
                if real(i, n + 2):
                    prepare_q(i, n + 2)
                if real(i, n - 2):
                    dve.wait_ge(logit_made, num(i, n - 1))
                    nc.vector.tensor_copy(logits[:, bass.ds(num(i, n - 2) * E, E)],
                                          logit_ps).then_inc(logit_ok, 1)
                if real(i, n - 1):
                    dve.wait_ge(rstd_ok, num(i, n + 3))
                    if real(i, n - 2):
                        dve.wait_ge(x2T_made, num(i, n - 1))
                    nc.vector.tensor_scalar(x2n[:, :], xin[last], mean2[:, 0:1], rstd[:, 1:2],
                                            ALU.subtract, ALU.mult).then_inc(x2n_ok, 1)
                if real(i, n):
                    dve.wait_ge(w1hi_ok, num(i, n + 1))
                    at = w1_at(i, n)
                    nc.vector.tensor_tensor(w1s[:, bass.ds(at + DC * H, H)], raw1[n % 2], w1s[:, bass.ds(at, H)],
                                            ALU.subtract).then_inc(w1lo_ok, 1)
                if real(i, n - 1):
                    dve.wait_ge(x2hi_ok, num(i, n))
                    nc.vector.tensor_tensor(x2split[last][:, D:2 * D], x2n[:, :], x2split[last][:, 0:D],
                                            ALU.subtract).then_inc(x2lo_ok, 1)
                if real(i, n + 2):
                    split_kq(i, n + 2)

            over_sequences(step)(dve)

            steps = 0

            def then(ins):
                nonlocal steps
                steps += 1
                ins.then_inc(route_step, 1)
                dve.wait_ge(route_step, steps)

            def by_sequence(ap):
                return ap.rearrange("p (b e) -> p b e", e=E)

            def over_experts(ap):
                return ap.unsqueeze(2).to_broadcast([P, B, E])

            below8 = cst[:, BELOW8:BELOW8 + E].unsqueeze(1).to_broadcast([P, B, E])
            dve.wait_ge(logit_ok, B)
            for choice in range(TOPK):
                left = logits if choice == 0 else others
                then(nc.vector.tensor_reduce(best[:, choice, :], by_sequence(left[:, :]), AX.X, ALU.max))
                then(nc.vector.tensor_tensor(by_sequence(ties[:, :]), by_sequence(left[:, :]),
                                             over_experts(best[:, choice, :]), ALU.is_equal))
                then(nc.vector.tensor_tensor(by_sequence(ties[:, :]), by_sequence(ties[:, :]), below8, ALU.mult))
                then(nc.vector.tensor_reduce(first[:, :], by_sequence(ties[:, :]), AX.X, ALU.min))
                then(nc.vector.tensor_tensor(onehot[:, choice, :, :], below8, over_experts(first[:, :]),
                                             ALU.is_equal))
                if choice == 0:
                    then(nc.vector.scalar_tensor_tensor(
                        out=others[:, :], in0=onehot[:, 0, :, :].rearrange("p b e -> p (b e)"), scalar=-3e38,
                        in1=logits[:, :], op0=ALU.mult, op1=ALU.add))
            nc.vector.tensor_tensor(gap[:, :], best[:, 1, :], best[:, 0, :], ALU.subtract).then_inc(gap_ok, 1)
            nc.vector.memset(chosen[:, B, :], 0.0).then_inc(chosen_ok, 1)
            nc.vector.tensor_tensor(chosen[:, 0:B, :], onehot[:, 0, :, :], onehot[:, 1, :, :],
                                    ALU.add).then_inc(chosen_ok, 1)
            dve.wait_ge(ratio_ok, 1)
            then(nc.vector.tensor_scalar(total[:, :], ratio[:, :], 1.0, None, ALU.add))
            then(nc.vector.reciprocal(inverse[:, :], total[:, :]))
            then(nc.vector.tensor_scalar(weight[:, 0:B], inverse[:, :], gate[:, 1:2], None, ALU.mult))
            then(nc.vector.tensor_tensor(weight[:, B:2 * B], weight[:, 0:B], ratio[:, :], ALU.mult))
            dve.wait_ge(rank_made, 1)
            then(nc.vector.tensor_scalar(count_i[:, :], rank_ps[:, B * E:(B + 1) * E], float(P - 1), None, ALU.add))
            nc.vector.tensor_scalar(parts_i[:, 0, :], count_i[:, :], 7, None, ALU.arith_shift_right)
            then(nc.vector.tensor_scalar(parts_i[:, 1, :], count_i[:, :], 8, None, ALU.arith_shift_right))
            then(nc.vector.tensor_copy(parts_f[:, :, :], parts_i[:, :, :]))
            then(nc.vector.tensor_tensor_scan(pair_end[:, :], twos, twos, 0.0, ALU.add, ALU.bypass))
            then(nc.vector.tensor_tensor(pair_start[:, :], pair_end[:, :], twos, ALU.subtract))
            then(nc.vector.tensor_scalar(pair_end[:, :], pair_end[:, :], float(PAIRS), None, ALU.min))
            then(nc.vector.tensor_scalar(pair_start[:, :], pair_start[:, :], float(PAIRS), None, ALU.min))
            then(nc.vector.tensor_tensor(paired[:, :], pair_end[:, :], pair_start[:, :], ALU.subtract))
            nc.vector.tensor_scalar(wide_base[:, :], pair_start[:, :], float(ROWS), None, ALU.mult)
            nc.vector.tensor_scalar(wide_rows[:, :], paired[:, :], float(ROWS), None, ALU.mult)
            then(nc.vector.scalar_tensor_tensor(out=single[:, :], in0=paired[:, :], scalar=-2.0, in1=units,
                                                op0=ALU.mult, op1=ALU.add))
            then(nc.vector.tensor_tensor_scan(single_end[:, :], single[:, :], single[:, :], 0.0, ALU.add, ALU.bypass))
            then(nc.vector.tensor_tensor(single_start[:, :], single_end[:, :], single[:, :], ALU.subtract))
            then(nc.vector.tensor_scalar(jump[:, :], single_start[:, :], float(2 * PAIRS), float(P), ALU.add, ALU.mult))
            then(nc.vector.tensor_tensor(jump[:, :], jump[:, :], wide_rows[:, :], ALU.subtract))
            then(nc.vector.tensor_tensor(jump[:, :], jump[:, :], wide_base[:, :], ALU.subtract))
            def each(ap):
                return ap.unsqueeze(1).to_broadcast([P, B, E])

            rank = rank_ps[:, 0:B * E].rearrange("p (b e) -> p b e", e=E)
            then(nc.vector.tensor_tensor(beyond[:, :, :], rank, each(wide_rows[:, :]), ALU.is_ge))
            nc.vector.tensor_tensor(slot[:, :, :], rank, each(wide_base[:, :]), ALU.add)
            then(nc.vector.tensor_tensor(beyond[:, :, :], beyond[:, :, :], each(jump[:, :]), ALU.mult))
            then(nc.vector.tensor_tensor(slot[:, :, :], slot[:, :, :], beyond[:, :, :], ALU.add))
            for choice in range(TOPK):
                then(nc.vector.tensor_tensor(slot_k[:, choice, :, :], onehot[:, choice, :, :], slot[:, :, :],
                                             ALU.mult))
            then(nc.vector.tensor_reduce(slots[:, :], slot_k[:, :, :, :].rearrange("p k b e -> p (k b) e"),
                                         AX.X, ALU.add))
            then(nc.vector.tensor_copy(slots_i[:, :], slots[:, :]))
            then(nc.vector.tensor_scalar(tile_i[:, :], slots_i[:, :], 7, None, ALU.arith_shift_right))
            then(nc.vector.tensor_copy(tile_f[:, :], tile_i[:, :]))
            nc.vector.scalar_tensor_tensor(out=lane_f[:, :], in0=tile_f[:, :], scalar=-float(P),
                                           in1=slots[:, :], op0=ALU.mult, op1=ALU.add).then_inc(lanes_ok, 1)

            def onto(ap, width):
                return ap.unsqueeze(2).to_broadcast([P, HOT, width])

            for c in range(HOTS):
                columns = slice(c * HOT, (c + 1) * HOT)
                if c >= 2:
                    dve.wait_ge(weight_hot_ok, c - 1)
                nc.vector.tensor_tensor(tile_eq[c % 2],
                                        cst[:, IOTA:IOTA + TCOLS].unsqueeze(1).to_broadcast([P, HOT, TCOLS]),
                                        onto(tile_f[:, columns], TCOLS), ALU.is_equal).then_inc(tile_eq_ok, 1)
                token = TOKEN1 + c * HOT % B
                dve.wait_ge(tile_eq_ok, c + 1)
                nc.vector.tensor_tensor(tile_hot[c][:, :, 0, :], tile_eq[c % 2], onto(cst[:, token:token + HOT], TCOLS),
                                        ALU.mult).then_inc(token_hot_ok, 1)
                if c == 0:
                    dve.wait_ge(lanes_ok, 1)
                nc.vector.tensor_tensor(lane_hot[c], cst[:, IOTA:IOTA + P].unsqueeze(1).to_broadcast([P, HOT, P]),
                                        onto(lane_f[:, columns], P), ALU.is_equal).then_inc(lane_hot_ok, 1)

            def ended(first, count, ends):
                return nc.vector.tensor_tensor(
                    tile_ge[:, first:first + count, :],
                    cst[0:1, IOTA:IOTA + count].unsqueeze(2).to_broadcast([1, count, E]),
                    ends[0:1, :].unsqueeze(1).to_broadcast([1, count, E]), ALU.is_ge)

            ended(0, PAIRS, pair_end)
            then(ended(PAIRS, SINGLES, single_end))
            then(nc.vector.tensor_reduce(tile_exp[:, :], tile_ge[:, :, :], AX.X, ALU.add))
            nc.vector.tensor_scalar(tile_expert[:, :], tile_exp[:, :], float(E - 1), None,
                                    ALU.min).then_inc(experts_ok, 1)
            dve.wait_ge(hot_used, HOTS)
            then(nc.vector.tensor_copy(table[:, :, :], table_ps[:, 0:2 * TCOLS]))
            then(nc.vector.tensor_scalar(row_less1[:, :], table[:, 0, :], -1.0, None, ALU.add))
            then(nc.vector.tensor_scalar(empty[:, :], table[:, 0, :], 0.0, cst[:, SPARE1:SPARE1 + 1],
                                         ALU.is_equal, ALU.mult))
            nc.vector.tensor_scalar(gather_row[:, :], row_less1[:, :], 0.0, None, ALU.max).then_inc(slots_ok, 1)
            nc.vector.tensor_tensor(scatter_row[:, :], row_less1[:, :], empty[:, :], ALU.add).then_inc(slots_ok, 1)

            def rows_transposed(tile):
                t, k, par, one = tile
                n = P if one else ROWS
                dve.wait_ge(rowsT_made, t + 1)
                nc.vector.tensor_copy(rowsT[par].rearrange("p s c n -> p (s c) n")[:, :, 0:n],
                                      t_ps[:, 0:4 * ROWS].rearrange("p (s n) -> p s n", s=4)[:, :, 0:n]
                                      ).then_inc(rowsT_ok, 1)

            dve.wait_ge(b2_in, 16)
            dve.wait_ge(experts_ok, 1)
            rows_transposed((0, 0, 0, False))

            def split(tile, pair):
                t, k, par, one = tile
                n = P if one else ROWS
                c = slice(2 * pair, 2 * pair + 2)
                piece = act32[:, 2 * pair * ROWS:2 * (pair + 1) * ROWS].rearrange("p (c n) -> p c n", c=2)[:, :, 0:n]
                dve.wait_ge(gelu_ok, 4 * t + pair + 1)
                nc.vector.tensor_copy(ghi[par][:, c, 0:n], piece).then_inc(ghi_ok, 1)
                dve.wait_ge(ghi_ok, 4 * t + pair + 1)
                nc.vector.tensor_tensor(glo[par][:, c, 0:n], piece, ghi[par][:, c, 0:n],
                                        ALU.subtract).then_inc(glo_ok, 1)

            def weigh(tile):
                t = tile[0]
                e = dve.value_load(tile_expert[0:1, bass.ds(t, 1)], min_val=0, max_val=E - 1)
                if tile_exists(shift(tile, -1)):
                    dve.wait_ge(yout_ok, parts(tile)[0][0])
                dve.wait_ge(y_made, t + 1)
                for unit, side, k in parts(tile):
                    nc.vector.tensor_tensor(ysum[side], y_ps[side][:, 0:D], b2bc[:, bass.ds(e * D, D)],
                                            ALU.add).then_inc(ysum_ok, 1)
                for unit, side, k in parts(tile):
                    dve.wait_ge(ysum_ok, unit + 1)
                    if not (isinstance(unit, int) and unit < 2):
                        dve.wait_ge(scattered[side], 16 * k)
                    nc.vector.tensor_scalar(yout[side], ysum[side], slot_gate[:, bass.ds(unit, 1)],
                                            None, ALU.mult).then_inc(yout_ok, 1)

            def step_c(tile):
                for pair in range(4):
                    split(tile, pair)
                    if pair == 2 and tile_exists(shift(tile, 1)):
                        rows_transposed(shift(tile, 1))
                if tile_exists(shift(tile, -1)):
                    weigh(shift(tile, -1))

            over_tiles(dve, step_c)
            weigh((TILES - 1, (TILES - 1) // 2, (TILES - 1) % 2, True))

        @block.tensor
        def _(pe):
            pe.wait_ge(const_in, 48)
            pe.wait_ge(halves_ok, 1)
            pe.wait_ge(pads_set, 1)
            identity_b = cstb[:, IDENT_B:IDENT_B + P]

            def transpose_kq(i, n):
                if real(i, n - 1):
                    pe.wait_ge(kqT_ok, num(i, n))
                pe.wait_ge(k_ok, num(i, n + 1))
                pe.wait_ge(q_ok, num(i, n + 1))
                for source, at in ((ksplit, 0), (qhi, 4)):
                    for g in range(4):
                        last = nc.tensor.transpose(kq_ps[:, (at + g) * P:(at + g + 1) * P],
                                                   source[:, 4 * g:4 * g + 4, :, :].rearrange("p h s d -> p (h s d)"),
                                                   identity_b)
                last.then_inc(kqT_made, 1)
                if real(i, n - 1):
                    pe.wait_ge(qlT_ok, num(i, n))
                for g in range(4):
                    last = nc.tensor.transpose(ql_ps[:, g * P:(g + 1) * P],
                                               qlo[:, 4 * g:4 * g + 4, :, :].rearrange("p h s d -> p (h s d)"),
                                               identity_b)
                last.then_inc(kqT_made, 1)

            def scores(i, n, which):
                t = num(i, n)
                pe.wait_ge(kqT_ok, t + 1)
                pe.wait_ge(qlT_ok, t + 1)
                for j in which:
                    rows = slice(32 * j, 32 * j + 32)
                    if real(i, n - 1):
                        if j == 0:
                            pe.wait_ge(outT_ok, t)
                        else:
                            pe.wait_ge(copied, 3 * t + j - 3)
                    for g in range(4):
                        to = sc_ps[j][:, g * P:(g + 1) * P]
                        nc.tensor.matmul(to, kqT[rows, 0, g, :], kqT[rows, 1, g, :], start=True, stop=False)
                        last = nc.tensor.matmul(to, kqT[rows, 0, g, :], kqT[rows, 2, g, :], start=False, stop=True)
                    last.then_inc(score_made, 1)

            def values(i, n):
                t = num(i, n)
                pe.wait_ge(s0_ok, t + 1)
                pe.wait_ge(selected, 3 * t + 3)
                for g in range(4):
                    for j in range(4):
                        h = 4 * g + j
                        last = nc.tensor.matmul(outT_ps[32 * j:32 * j + 32, g * P:(g + 1) * P],
                                                context[:, n % SLOTS, h * HD:h * HD + 32], smask[j][:, g, :],
                                                start=True, stop=True)
                last.then_inc(outT_made, 1)

            def transpose_outputs(i, n):
                pe.wait_ge(outT_ok, num(i, n + 1))
                if real(i, n - 1):
                    pe.wait_ge(x1_ok, num(i, n))
                for j in range(4):
                    last = nc.tensor.transpose(o_ps[:, j * P:(j + 1) * P], outT[:, j * P:(j + 1) * P],
                                               cst[:, IDENT:IDENT + P])
                last.then_inc(out_made, 1)

            def transpose_normed(i, n):
                pe.wait_ge(x2n_ok, num(i, n + 1))
                for d in range(DC):
                    last = nc.tensor.transpose(r_ps[:, d * P:(d + 1) * P], x2n[:, d * P:(d + 1) * P],
                                               cst[:, IDENT:IDENT + P])
                last.then_inc(x2T_made, 1)

            def router(i, n):
                pe.wait_ge(x2T_ok, num(i, n + 1))
                for d in range(DC):
                    last = nc.tensor.matmul(logit_ps, x2T[:, d, :], rw[:, d, :],
                                            start=(d == 0), stop=(d == DC - 1))
                last.then_inc(logit_made, 1)

            def step(i, n):
                if real(i, n):
                    scores(i, n, (1, 2, 3))
                if real(i, n - 1):
                    transpose_outputs(i, n - 1)
                if real(i, n):
                    scores(i, n, (0,))
                if real(i, n - 2):
                    transpose_normed(i, n - 2)
                if real(i, n + 1):
                    transpose_kq(i, n + 1)
                if real(i, n - 2):
                    router(i, n - 2)
                if real(i, n):
                    values(i, n)

            over_sequences(step)(pe)

            pe.wait_ge(chosen_ok, 2)
            for ahead in range(1, B + 1):
                nc.tensor.matmul(rank_ps[:, ahead * E:(B + 1) * E], cstb[:, ONES_B:ONES_B + P],
                                 chosen[:, 0:B + 1 - ahead, :].rearrange("p b e -> p (b e)"),
                                 start=(ahead == 1), stop=False, skip_group_check=True)
            last = nc.tensor.matmul(rank_ps[:, 0:(B + 1) * E], cstb[:, BEFORE_B:BEFORE_B + P],
                                    chosen[:, :, :].rearrange("p b e -> p (b e)"),
                                    start=False, stop=True, skip_group_check=True)
            last.then_inc(rank_made, 1)

            for c in range(HOTS):
                pe.wait_ge(token_hot_ok, c + 1)
                pe.wait_ge(weight_hot_ok, c + 1)
                pe.wait_ge(lane_hot_ok, c + 1)
                for n in range(HOT):
                    last = nc.tensor.matmul(table_ps[:, 0:2 * TCOLS], lane_hot[c][:, n, :],
                                            tile_hot[c][:, n, :, :].rearrange("p a l -> p (a l)"),
                                            start=(c == 0 and n == 0), stop=(c == HOTS - 1 and n == HOT - 1))
                last.then_inc(hot_used, 1)

            def transpose_rows(tile):
                t, k, par, one = tile
                pe.wait_ge(gathered[par], 16 * units_of_parity_through(tile))
                if tile_exists(shift(tile, -1)):
                    pe.wait_ge(rowsT_ok, t)
                for n in range(4):
                    for half in range(len(parts(tile))):
                        at = n * ROWS + half * P
                        last = nc.tensor.transpose(t_ps[:, at:at + P], rows_in[par][:, half, n * P:(n + 1) * P],
                                                   identity_b)
                last.then_inc(rowsT_made, 1)

            def hidden(tile):
                t, k, par, one = tile
                rows = P if one else ROWS
                e = expert(t)
                pe.wait_ge(rowsT_ok, t + 1)
                for c in range(HC):
                    if c % 2 == 0 and tile_exists(shift(tile, -1)):
                        pe.wait_ge(gelu_ok, 4 * t - 3 + c // 2)
                    n = 0
                    for wpart, xpart in ((0, 0), (0, 1), (1, 0)):
                        for d in range(DC):
                            last = nc.tensor.matmul(
                                h_ps[c // 2][:, c % 2 * ROWS:c % 2 * ROWS + rows],
                                w1s[:, bass.ds(e * (2 * DC * H) + (wpart * DC + d) * H + c * P, P)],
                                rowsT[par][:, xpart, d, 0:rows], start=(n == 0), stop=(n == 3 * DC - 1))
                            n += 1
                    if c % 2 == 1:
                        last.then_inc(h_made, 1)

            def output(tile):
                t, k, par, one = tile
                e = expert(t)
                if tile_exists(shift(tile, -1)):
                    pe.wait_ge(ysum_ok, parts(tile)[0][0])
                for c in range(HC):
                    if c % 2 == 0:
                        pe.wait_ge(glo_ok, 4 * t + c // 2 + 1)
                    for half, (unit, side, _) in enumerate(parts(tile)):
                        rows = slice(half * P, (half + 1) * P)
                        for gpart, wpart in ((ghi, 0), (glo, 0), (ghi, 1)):
                            last = nc.tensor.matmul(
                                y_ps[side][:, 0:D], gpart[par][:, c, rows],
                                w2s[:, bass.ds(e * (2 * HC * D) + (wpart * HC + c) * D, D)],
                                start=(c == 0 and wpart == 0 and gpart is ghi), stop=(c == HC - 1 and wpart == 1))
                last.then_inc(y_made, 1)

            def expert(t):
                return pe.value_load(tile_expert[0:1, bass.ds(t, 1)], min_val=0, max_val=E - 1)

            pe.wait_ge(experts_ok, 1)
            pe.wait_ge(w1lo_ok, B)
            pe.wait_ge(w2lo_ok, B)
            start = (0, 0, 0, False)
            transpose_rows(start)
            hidden(start)
            transpose_rows(shift(start, 1))

            def step_c(tile):
                if tile_exists(shift(tile, 1)):
                    hidden(shift(tile, 1))
                if tile_exists(shift(tile, 2)):
                    transpose_rows(shift(tile, 2))
                output(tile)

            over_tiles(pe, step_c)


def kernel(x, ctx_1024, g_xattn, g_ffn, L0_ffn_router_w, L0_ffn_w1, L0_ffn_b1, L0_ffn_w2, L0_ffn_b2):
    import concourse.bacc as bacc
    from concourse.bass_utils import run_bass_kernel_spmd

    const, const_b = constants()
    arrays = {
        "x_in": np.ascontiguousarray(x),
        "ctx_in": np.ascontiguousarray(ctx_1024),
        "gates_in_": np.concatenate([np.asarray(g_xattn), np.asarray(g_ffn)]).reshape(1, 2),
        "router_in": np.ascontiguousarray(L0_ffn_router_w),
        "w1_in": np.ascontiguousarray(L0_ffn_w1),
        "b1_in": np.ascontiguousarray(np.asarray(L0_ffn_b1).reshape(E * HC, P).T),
        "w2_in": np.ascontiguousarray(L0_ffn_w2),
        "b2_in_": np.ascontiguousarray(np.asarray(L0_ffn_b2).reshape(1, E * D)),
        "const_in_": const,
        "const_b_in_": const_b,
    }
    nc = bacc.Bacc("TRN2", target_bir_lowering=False, num_devices=1)
    args = [nc.dram_tensor(n, a.shape, mybir.dt.from_np(a.dtype), kind="ExternalInput").ap() for n, a in arrays.items()]
    out = nc.dram_tensor("out_rows", [TOKENS + SPARE, D], F32, kind="ExternalOutput").ap()
    build(nc, *args, out)
    result = run_bass_kernel_spmd(nc, [arrays], core_ids=[0])
    return result.results[0]["out_rows"][:TOKENS].reshape(B, S, D)
```

```python
import math
from contextlib import ExitStack

import numpy as np

import concourse.bass as bass
from concourse import mybir

ALU = mybir.AluOpType
ACT = mybir.ActivationFunctionType
AX = mybir.AxisListType
F32 = mybir.dt.float32
BF16 = mybir.dt.bfloat16
I32 = mybir.dt.int32

P = 128
B, S, D = 16, 128, 256
HEADS, HD = 16, 16
E, H, TOPK = 8, 1024, 2
TOKENS = B * S
DC = D // P
HC = H // P
UNITS = TOKENS * TOPK // P + E - 1
PAIRS = (UNITS - E) // 2
SINGLES = max(E, UNITS - 2 * PAIRS)
TILES = PAIRS + SINGLES
UNITS_RUN = 2 * PAIRS + SINGLES
TCOLS = UNITS_RUN + UNITS_RUN % 2
ROWS = 2 * P
EPS = 1e-5
SLOTS = 4
HOT = 4
HOTS = TOPK * B // HOT
SPARE = P

CQ, SQ, CK, SK = 0, D, 2 * D, 3 * D
IDENT = 4 * D
CAUSAL = IDENT + P
IOTA = CAUSAL + P
TOKEN1 = IOTA + P
SPARE1 = TOKEN1 + B
BELOW8 = SPARE1 + 1
NCONST = BELOW8 + E
IDENT_B, BEFORE_B, ONES_B, NCONST_B = 0, P, 2 * P, 3 * P


def constants():
    half = HD // 2
    base = (np.arange(0, HD, 2, dtype=np.float32) + np.float32(0.4 * HD)) / np.float32(1.4 * HD)
    pos = np.arange(S, dtype=np.float64)
    scale = base.astype(np.float64)[None, :] ** (pos / 512.0)[:, None]
    freq = (1.0 / 10000.0 ** (np.arange(half, dtype=np.float32) / np.float32(half))).astype(np.float32)
    angle = (pos[:, None].astype(np.float32) * freq[None, :]).astype(np.float64)
    gamma = (1.0 - np.exp(np.linspace(math.log(1 / 32), math.log(1 / 512), HEADS))).astype(np.float32)
    decay = gamma.astype(np.float64)[None, :] ** pos[:, None]
    c = np.zeros((P, NCONST), np.float32)
    for at_cos, at_sin, factor in ((CQ, SQ, decay[:, :, None] * scale[:, None, :]),
                                   (CK, SK, 1 / (decay[:, :, None] * scale[:, None, :]))):
        cos = np.cos(angle)[:, None, :] * factor
        sin = np.sin(angle)[:, None, :] * factor
        c[:, at_cos:at_cos + D] = np.stack([cos, cos], -1).reshape(S, D)
        c[:, at_sin:at_sin + D] = np.stack([-sin, sin], -1).reshape(S, D)
    c[:, IDENT:IDENT + P] = np.eye(P)
    c[:, CAUSAL:CAUSAL + P] = np.triu(np.ones((P, P)))
    c[:, IOTA:IOTA + P] = np.arange(P)
    c[:, TOKEN1:TOKEN1 + B] = 1 + np.arange(P)[:, None] + P * np.arange(B)
    c[:, SPARE1] = 1 + TOKENS + np.arange(P)
    c[:, BELOW8:BELOW8 + E] = np.arange(E) - E
    cb = np.zeros((P, NCONST_B), np.float32)
    cb[:, IDENT_B:IDENT_B + P] = np.eye(P)
    cb[:, BEFORE_B:BEFORE_B + P] = np.triu(np.ones((P, P)), 1)
    cb[:, ONES_B:ONES_B + P] = 1
    return c, cb


def swapped(ap):
    return ap.rearrange("p (a b) -> p a b", b=2)[:, :, ::-1]


def pairs(ap):
    return ap.rearrange("p (a b) -> p a b", b=2)


def build(nc, x, ctx, gates, router_w, w1, b1, w2, b2, const, const_b, out):
    with ExitStack() as stack:
        def sb(name, shape, dt):
            return stack.enter_context(nc.sbuf_tensor(name, shape, dt))

        def psum(name, shape, dt=F32):
            return stack.enter_context(nc.psum_tensor(name, shape, dt))

        def sem(name):
            return stack.enter_context(nc.semaphore(name))

        def sem2(name):
            return [sem(f"{name}{par}") for par in range(2)]

        x_rows = x.rearrange("b s d -> (b s) d")
        ctx_rows = ctx.rearrange("b s d -> (b s) d")
        w1_rows = w1.rearrange("e d h -> (e d) h")
        w2_rows = w2.rearrange("e h d -> (e h) d")
        normed_dram = nc.dram_tensor("normed_rows", [TOKENS, 2 * D], BF16, kind="Internal").ap()

        cst = sb("cst", [P, NCONST], F32)
        cstb = sb("cstb", [P, NCONST_B], BF16)
        gate = sb("gate", [P, 2], F32)
        minus_half = sb("minus_half", [P, 2], F32)
        rw = sb("rw", [P, DC, E], F32)
        b1c = sb("b1c", [P, E * HC], F32)
        zero_rows = sb("zero_rows", [P, D], F32)
        w1s = sb("w1s", [P, E * 2 * DC * H], BF16)
        w2s = sb("w2s", [P, E * 2 * HC * D], BF16)
        raw = sb("raw", [P, 4 * H], F32)
        raw1 = [raw[:, par * H:(par + 1) * H] for par in range(2)]
        raw2 = [raw[:, (2 + par) * H:(3 + par) * H] for par in range(2)]
        b2bc = raw[:, 0:E * D]
        act32 = raw[:, E * D:E * D + HC * ROWS]

        seq_in = sb("seq_in", [P, SLOTS * D], F32)
        context = sb("context", [P, SLOTS, D + HD], F32)
        xin = [seq_in[:, s * D:(s + 1) * D] for s in range(SLOTS)]
        cin = [context[:, s, 0:D] for s in range(SLOTS)]
        stats = sb("stats", [P, 6], F32)
        moments = sb("moments", [P, 2, 2], F32)
        mean1, mean2 = moments[:, 0, :], moments[:, 1, :]
        veps = sb("veps", [P, 2], F32)
        rstd = sb("rstd", [P, 2], F32)
        rotary = sb("rotary", [P, 5 * D], F32)
        xn, turn, kturn, qrot, krot = (rotary[:, n * D:(n + 1) * D] for n in range(5))
        ksplit = sb("ksplit", [P, HEADS, 4, HD], BF16)
        qsplit = sb("qsplit", [P, HEADS, 4, HD], BF16)
        kT = sb("kT", [P, HEADS // 2, P], BF16)
        qT = sb("qT", [P, HEADS // 2, P], BF16)
        masked = sb("masked", [P, 4 * 4 * P], F32)
        smask = [masked[:, 4 * j * P:4 * (j + 1) * P].rearrange("p (g n) -> p g n", g=4) for j in range(4)]
        halves = masked[:, 0:NCONST_B]
        stats2 = sb("stats2", [P, 6], F32)
        x2n = sb("x2n", [P, D], F32)
        x2split = [sb(f"x2split{s}", [P, 2 * D], BF16) for s in range(SLOTS)]
        x2T = sb("x2T", [P, DC, P], F32)
        outT = sb("outT", [P, 4 * P], F32)

        logits = sb("logits", [P, B * E], F32)
        others = sb("others", [P, B * E], F32)
        ties = sb("ties", [P, B * E], F32)
        first = sb("first", [P, B], F32)
        best = sb("best", [P, TOPK, B], F32)
        onehot = sb("onehot", [P, TOPK, B, E], F32)
        chosen = sb("chosen", [P, B + 1, E], BF16)
        count_i = sb("count_i", [P, E], I32)
        parts_i = sb("parts_i", [P, 2, E], I32)
        parts_f = sb("parts_f", [P, 2, E], F32)
        units, twos = parts_f[:, 0, :], parts_f[:, 1, :]
        pair_end = sb("pair_end", [P, E], F32)
        pair_start = sb("pair_start", [P, E], F32)
        paired = sb("paired", [P, E], F32)
        single = sb("single", [P, E], F32)
        single_end = sb("single_end", [P, E], F32)
        single_start = sb("single_start", [P, E], F32)
        wide_base = sb("wide_base", [P, E], F32)
        wide_rows = sb("wide_rows", [P, E], F32)
        jump = sb("jump", [P, E], F32)
        slot = sb("slot", [P, B, E], F32)
        beyond = sb("beyond", [P, B, E], F32)
        slot_k = sb("slot_k", [P, TOPK, B, E], F32)
        slots = sb("slots", [P, TOPK * B], F32)
        slots_i = sb("slots_i", [P, TOPK * B], I32)
        tile_i = sb("tile_i", [P, TOPK * B], I32)
        tile_f = sb("tile_f", [P, TOPK * B], F32)
        lane_f = sb("lane_f", [P, TOPK * B], F32)
        gap = sb("gap", [P, B], F32)
        ratio = sb("ratio", [P, B], F32)
        total = sb("total", [P, B], F32)
        inverse = sb("inverse", [P, B], F32)
        weight = sb("weight", [P, TOPK * B], F32)
        table = sb("table", [P, 2, TCOLS], F32)
        slot_gate = table[:, 1, :]
        row_less1 = sb("row_less1", [P, TCOLS], F32)
        empty = sb("empty", [P, TCOLS], F32)
        gather_row = sb("gather_row", [P, TCOLS], I32)
        scatter_row = sb("scatter_row", [P, TCOLS], I32)
        gather_now = [[sb(f"gather_now{p}{half}", [P, 1], I32) for half in range(2)] for p in range(2)]
        scatter_now = [sb(f"scatter_now{half}", [P, 1], I32) for half in range(2)]
        tile_ge = sb("tile_ge", [1, TILES, E], F32)
        tile_exp = sb("tile_exp", [1, TILES], F32)
        tile_expert = sb("tile_expert", [1, TILES], I32)

        rows_in = [seq_in[:, 2 * p * D:2 * (p + 1) * D].bitcast(BF16).rearrange("p (h d) -> p h d", h=2)
                   for p in range(2)]
        rowsT = [rotary[:, 2 * p * D:2 * (p + 1) * D].bitcast(BF16).rearrange("p (s c n) -> p s c n", s=2, c=DC)
                 for p in range(2)]
        gelu_even = sb("gelu_even", [P, 2, HC, ROWS], BF16)
        gelu_odd = masked[:, :].bitcast(BF16).rearrange("p (s c n) -> p s c n", s=2, c=HC)
        ghi = [gelu_even[:, 0, :, :], gelu_odd[:, 0, :, :]]
        glo = [gelu_even[:, 1, :, :], gelu_odd[:, 1, :, :]]
        lane_hot = [raw[:, c * HOT * P:(c + 1) * HOT * P].rearrange("p (n l) -> p n l", n=HOT) for c in range(HOTS)]
        room = [masked[:, :], gelu_even[:, :, :, :].rearrange("p s c n -> p (s c n)").bitcast(F32)]
        width = HOT * TCOLS
        tile_hot = [room[c % 2][:, c // 2 * 2 * width:(c // 2 + 1) * 2 * width].rearrange("p (n a l) -> p n a l",
                                                                                          n=HOT, a=2)
                    for c in range(HOTS)]
        tile_eq = [room[c][:, HOTS * width:(HOTS + 1) * width].rearrange("p (n l) -> p n l", n=HOT) for c in range(2)]
        ysum = [cin[half] for half in range(2)]
        yout = [cin[2 + half] for half in range(2)]

        bank = [psum(f"bank{n}", [P, 512]) for n in range(8)]
        sc_ps = bank[0:4]
        kT_ps = bank[4][:, :].bitcast(BF16)
        qT_ps = bank[5][:, :].bitcast(BF16)
        outT_ps = bank[0]
        o_ps = bank[6]
        r_ps = bank[7]
        logit_ps = r_ps[:, D:D + E]
        rank_ps = bank[0]
        table_ps = bank[1]
        h_ps = bank[0:4]
        t_ps = bank[4][:, :].bitcast(BF16)
        y_ps = [bank[5], bank[6]]

        const_in, gates_in, b2_in = sem("const_in"), sem("gates_in"), sem("b2_in")
        zeros_set, zeros_out = sem("zeros_set"), sem("zeros_out")
        half_set, gates_ready, halves_ok = sem("half_set"), sem("gates_ready"), sem("halves_ok")
        halves_in = sem("halves_in")
        xc_in, raw_in = [sem(f"xc_in{s}") for s in range(SLOTS)], sem2("raw_in")
        stats1_ok, mean1_ok, stats2_ok, mean2_ok = sem("stats1_ok"), sem("mean1_ok"), sem("stats2_ok"), sem("mean2_ok")
        veps_ok, rstd_ok = sem("veps_ok"), sem("rstd_ok")
        kterms, krot_ok, khi_ok, k_ok = sem("kterms"), sem("krot_ok"), sem("khi_ok"), sem("k_ok")
        xn_ok, qterms, qrot_ok, qhi_ok, q_ok = sem("xn_ok"), sem("qterms"), sem("qrot_ok"), sem("qhi_ok"), sem("q_ok")
        kT_made, qT_made, kT_ok, qT_ok = sem("kT_made"), sem("qT_made"), sem("kT_ok"), sem("qT_ok")
        score_made = sem("score_made")
        s0_ok, copied, selected = sem("s0_ok"), sem("copied"), sem("selected")
        pads_set, outT_made, outT_ok, out_made = sem("pads_set"), sem("outT_made"), sem("outT_ok"), sem("out_made")
        x1_ok = sem("x1_ok")
        x1_out, x2_out = sem2("x1_out"), sem2("x2_out")
        x2n_ok, x2hi_ok, x2lo_ok = sem("x2n_ok"), sem("x2hi_ok"), sem("x2lo_ok")
        x2T_made, x2T_ok, logit_made, logit_ok = sem("x2T_made"), sem("x2T_ok"), sem("logit_made"), sem("logit_ok")
        w1hi_ok, w1lo_ok, w2hi_ok, w2lo_ok = sem("w1hi_ok"), sem("w1lo_ok"), sem("w2hi_ok"), sem("w2lo_ok")
        route_step, chosen_ok, rank_made = sem("route_step"), sem("chosen_ok"), sem("rank_made")
        gap_ok, ratio_ok = sem("gap_ok"), sem("ratio_ok")
        lanes_ok, lane_hot_ok, tile_eq_ok = sem("lanes_ok"), sem("lane_hot_ok"), sem("tile_eq_ok")
        token_hot_ok, weight_hot_ok, hot_used = sem("token_hot_ok"), sem("weight_hot_ok"), sem("hot_used")
        experts_ok, slots_ok = sem("experts_ok"), sem("slots_ok")
        gathered, scattered = sem2("gathered"), sem2("scattered")
        gather_set, scatter_set = sem("gather_set"), sem("scatter_set")
        rowsT_made, rowsT_ok = sem("rowsT_made"), sem("rowsT_ok")
        h_made, gelu_ok, ghi_ok, glo_ok = sem("h_made"), sem("gelu_ok"), sem("ghi_ok"), sem("glo_ok")
        y_made, ybias_ok, ysum_ok, yout_ok = sem("y_made"), sem("ybias_ok"), sem("ysum_ok"), sem("yout_ok")

        block = stack.enter_context(nc.Block())

        def over_sequences(step):
            def run(eng):
                for n in range(-2, 2):
                    step(0, n)
                with eng.Fori(0, B // SLOTS - 1) as i:
                    for n in range(2, 2 + SLOTS):
                        step(i, n)
                for n in range(B - 2, B + 2):
                    step(0, n)
            return run

        def real(i, n):
            return not isinstance(i, int) or 0 <= n < B

        def num(i, n):
            return SLOTS * i + n

        def half_num(i, n):
            return SLOTS // 2 * i + n // 2

        def w1_at(i, n):
            return half_num(i, n) * (2 * DC * H) + n % 2 * H

        def w2_at(i, n):
            return half_num(i, n) * (2 * HC * D) + n % 2 * (2 * H)

        def w2_part(at, part):
            return w2s[:, bass.ds(at, 2 * H)].rearrange("p (c s d) -> p c s d", s=2, d=D)[:, :, part, :]

        def chunks(ap):
            return ap.rearrange("p (c d) -> p c d", d=D)

        def twice(ap):
            return ap.rearrange("p (h d) -> p h d", d=HD).unsqueeze(2).to_broadcast([P, HEADS, 2, HD])

        def own(eng, sem, value):
            if not isinstance(value, int):
                value = eng.lower_val(value)
            eng.wait_ge(const_in, 48)
            eng.wait_ge(sem, value)

        def shift(tile, by):
            t, k, par, one = tile
            return t + by, k + (par + by) // 2, (par + by) % 2, (t + by >= PAIRS if isinstance(t, int) else one)

        def tile_exists(tile):
            return not isinstance(tile[0], int) or 0 <= tile[0] < TILES

        def parts(tile):
            t, k, par, one = tile
            if one:
                return [(t + PAIRS, (par + PAIRS) % 2, k + (par + PAIRS) // 2)]
            return [(2 * t, 0, t), (2 * t + 1, 1, t)]

        def units_through(tile):
            return parts(tile)[-1][0] + 1

        def units_of_parity_through(tile):
            t, k, par, one = tile
            return k + 1 + (PAIRS + 1 - par) // 2 if one else 2 * (k + 1)

        def over_tiles(eng, step, at_bounds=lambda: None):
            def peeled(first, last):
                for t in range(first, last):
                    step((t, t // 2, t % 2, t >= PAIRS))

            def looped(first, last, one):
                at_bounds()
                with eng.Fori(first // 2, last // 2) as i:
                    step((2 * i, i, 0, one))
                    step((2 * i + 1, i, 1, one))
                at_bounds()

            wide_last = (PAIRS - 3) // 2 * 2
            single_first = (PAIRS + 2) // 2 * 2
            single_last = (TILES - 3) // 2 * 2
            peeled(0, 2)
            looped(2, wide_last, False)
            peeled(wide_last, single_first)
            looped(single_first, single_last, True)
            peeled(single_last, TILES)

        @block.sync
        def _(sp):
            def load_seq(i, n):
                rows = bass.ds(num(i, n) * P, P)
                sp.dma_start(xin[n % SLOTS], x_rows[rows, :]).then_inc(xc_in[n % SLOTS], 16)
                sp.dma_start(cin[n % SLOTS], ctx_rows[rows, :]).then_inc(xc_in[n % SLOTS], 16)

            def load_raw(i, n):
                sp.dma_start(raw1[n % 2], w1_rows[bass.ds(num(i, n) * P, P), :]).then_inc(raw_in[n % 2], 16)
                sp.dma_start(raw2[n % 2].rearrange("p (c d) -> p c d", c=4),
                             w2_rows[bass.ds(num(i, n) * 4 * P, 4 * P), :].rearrange("(c p) d -> p c d", p=P)
                             ).then_inc(raw_in[n % 2], 16)

            load_seq(0, 0)
            sp.dma_start(cst[:, :], const).then_inc(const_in, 16)
            sp.dma_start(halves[:, :], const_b).then_inc(halves_in, 16)
            sp.dma_start(gate[:, :], gates.to_broadcast([P, 2])).then_inc(gates_in, 16)
            sp.dma_start(rw[:, :, :], router_w.rearrange("(c p) e -> p c e", p=P)).then_inc(const_in, 16)
            sp.dma_start(b1c[:, :], b1).then_inc(const_in, 16)
            load_seq(0, 1)
            load_raw(0, 0)
            load_seq(0, 2)
            load_raw(0, 1)
            load_seq(0, 3)
            sp.wait_ge(zeros_set, 1)
            sp.dma_start(out[TOKENS:TOKENS + SPARE, :], zero_rows[:, :]).then_inc(zeros_out, 16)

            def step(i, n):
                if real(i, n - 2):
                    if real(i, n + 2):
                        sp.wait_ge(x2n_ok, num(i, n - 1))
                        sp.wait_ge(x1_out[n % 2], 16 * half_num(i, n))
                        load_seq(i, n + 2)
                    sp.wait_ge(x2lo_ok, num(i, n - 1))
                    sp.dma_start(normed_dram[bass.ds(num(i, n - 2) * P, P), :],
                                 x2split[(n - 2) % SLOTS][:, :]).then_inc(x2_out[n % 2], 16)
                if real(i, n - 1):
                    sp.wait_ge(x1_ok, num(i, n))
                    sp.dma_start(out[bass.ds(num(i, n - 1) * P, P), :],
                                 xin[(n - 1) % SLOTS]).then_inc(x1_out[(n - 1) % 2], 16)
                    if real(i, n + 1):
                        if real(i, n - 2):
                            sp.wait_ge(x2_out[n % 2], 16 * half_num(i, n))
                        sp.wait_ge(w1lo_ok, num(i, n))
                        sp.wait_ge(w2lo_ok, num(i, n))
                        load_raw(i, n + 1)

            over_sequences(step)(sp)
            sp.wait_ge(hot_used, HOTS // 2)
            sp.dma_start(b2bc, b2.to_broadcast([P, E * D])).then_inc(b2_in, 16)
            sp.wait_ge(scattered[0], 16 * ((UNITS_RUN + 1) // 2))
            sp.wait_ge(scattered[1], 16 * (UNITS_RUN // 2))

        @block.gpsimd
        def _(pool):
            pool.memset(zero_rows[:, :], 0.0).then_inc(zeros_set, 1)
            pool.memset(context[:, :, D:D + HD], 0.0).then_inc(pads_set, 1)
            pool.memset(minus_half[:, :], -0.5).then_inc(half_set, 1)
            pool.wait_ge(half_set, 1)

            def inverse_roots(i, n):
                one, two = real(i, n + 2), real(i, n - 1)
                columns = slice(0 if one else 1, 2 if two else 1)
                if one:
                    own(pool, mean1_ok, num(i, n + 3))
                if two:
                    own(pool, mean2_ok, num(i, n))
                pool.tensor_scalar(veps[:, columns], moments[:, columns, 1], EPS, None, ALU.add).then_inc(veps_ok, 1)
                pool.wait_ge(veps_ok, num(i, n + 3))
                pool.tensor_tensor(rstd[:, columns], veps[:, columns], minus_half[:, columns],
                                   ALU.pow).then_inc(rstd_ok, 1)

            def select(i, n, j):
                own(pool, copied, 3 * num(i, n) + j)
                pool.affine_select(out=smask[j], in_=smask[j], compare_op=ALU.is_ge, fill=0.0, base=0,
                                   pattern=[[0, 4], [1, P]], channel_multiplier=-1).then_inc(selected, 1)

            def step(i, n):
                if real(i, n):
                    for j in range(1, 4):
                        select(i, n, j)
                if real(i, n + 2) or real(i, n - 1):
                    inverse_roots(i, n)
                if real(i, n + 2):
                    pool.wait_ge(khi_ok, num(i, n + 3))
                    pool.tensor_tensor(ksplit[:, :, 1::2, :], twice(krot), ksplit[:, :, 0::2, :],
                                       ALU.subtract).then_inc(k_ok, 1)
                if real(i, n):
                    pool.wait_ge(w2hi_ok, num(i, n + 1))
                    at = w2_at(i, n)
                    pool.tensor_tensor(w2_part(at, 1), chunks(raw2[n % 2]), w2_part(at, 0),
                                       ALU.subtract).then_inc(w2lo_ok, 1)

            over_sequences(step)(pool)

            def gather(tile):
                par = tile[2]
                for half, (unit, _, _) in enumerate(parts(tile)):
                    pool.tensor_copy(gather_now[par][half][:, :],
                                     gather_row[:, bass.ds(unit, 1)]).then_inc(gather_set, 1)
                    own(pool, gather_set, unit + 1)
                    pool.indirect_dma_start(
                        out=rows_in[par][:, half, :], out_offset=None, in_=normed_dram,
                        in_offset=bass.IndirectOffsetOnAxis(ap=gather_now[par][half][:, :], axis=0),
                        bounds_check=TOKENS - 1).then_inc(gathered[par], 16)

            for c in range(HOTS):
                pool.wait_ge(tile_eq_ok, c + 1)
                pool.tensor_tensor(tile_hot[c][:, :, 1, :], tile_eq[c % 2],
                                   weight[:, c * HOT:(c + 1) * HOT].unsqueeze(2).to_broadcast([P, HOT, TCOLS]),
                                   ALU.mult).then_inc(weight_hot_ok, 1)
            pool.wait_ge(slots_ok, 2)
            for par in range(2):
                pool.wait_ge(x2_out[par], 16 * (B // 2))
                pool.wait_ge(x1_out[par], 16 * (B // 2))
            pool.wait_ge(zeros_out, 16)
            start = (0, 0, 0, False)
            gather(start)
            gather(shift(start, 1))
            pool.wait_ge(rowsT_made, 1)
            gather(shift(start, 2))

            def step_c(tile):
                if tile_exists(shift(tile, 3)):
                    pool.wait_ge(rowsT_made, tile[0] + 2)
                    gather(shift(tile, 3))
                for unit, side, k in parts(tile):
                    pool.tensor_copy(scatter_now[side][:, :],
                                     scatter_row[:, bass.ds(unit, 1)]).then_inc(scatter_set, 1)
                    own(pool, scatter_set, unit + 1)
                    pool.wait_ge(yout_ok, unit + 1)
                    if not (isinstance(unit, int) and unit == 0):
                        own(pool, scattered[1 - side], 16 * (k + side))
                    pool.indirect_dma_start(
                        out=out, out_offset=bass.IndirectOffsetOnAxis(ap=scatter_now[side][:, :], axis=0),
                        in_=yout[side], in_offset=None, bounds_check=TOKENS + SPARE - 1,
                        compute_op=ALU.add).then_inc(scattered[side], 16)

            over_tiles(pool, step_c)

        @block.scalar
        def _(act):
            act.wait_ge(gates_in, 16)
            nc.scalar.activation(gate[:, :], gate[:, :], ACT.Tanh).then_inc(gates_ready, 1)
            act.wait_ge(halves_in, 16)
            nc.scalar.copy(cstb[:, :], halves[:, :]).then_inc(halves_ok, 1)

            def step(i, n):
                if real(i, n):
                    for j in range(1, 4):
                        act.wait_ge(score_made, 4 * num(i, n) + j)
                        nc.scalar.copy(smask[j], sc_ps[j][:, :]).then_inc(copied, 1)
                if real(i, n - 2):
                    act.wait_ge(x2T_made, num(i, n - 1))
                    nc.scalar.copy(x2T[:, :, :], r_ps[:, 0:D]).then_inc(x2T_ok, 1)
                if real(i, n + 1):
                    act.wait_ge(kT_made, num(i, n + 2))
                    nc.scalar.copy(kT[:, :, :], kT_ps[:, 0:8 * P]).then_inc(kT_ok, 1)
                    act.wait_ge(qT_made, num(i, n + 2))
                    nc.scalar.copy(qT[:, :, :], qT_ps[:, 0:8 * P]).then_inc(qT_ok, 1)
                if real(i, n):
                    act.wait_ge(raw_in[n % 2], 32 * (half_num(i, n) + 1))
                    nc.scalar.copy(w2_part(w2_at(i, n), 0), chunks(raw2[n % 2])).then_inc(w2hi_ok, 1)
                if real(i, n + 2):
                    act.wait_ge(krot_ok, num(i, n + 3))
                    nc.scalar.copy(ksplit[:, :, 0::2, :], twice(krot)).then_inc(khi_ok, 1)
                if real(i, n):
                    nc.scalar.copy(w1s[:, bass.ds(w1_at(i, n), H)], raw1[n % 2]).then_inc(w1hi_ok, 1)
                    act.wait_ge(outT_made, num(i, n + 1))
                    if real(i, n - 1):
                        act.wait_ge(out_made, num(i, n))
                    nc.scalar.copy(outT[:, :], outT_ps[:, :]).then_inc(outT_ok, 1)
                if real(i, n - 1):
                    act.wait_ge(x2n_ok, num(i, n))
                    nc.scalar.copy(x2split[(n - 1) % SLOTS][:, 0:D], x2n[:, :]).then_inc(x2hi_ok, 1)
                if real(i, n + 2):
                    act.wait_ge(qrot_ok, num(i, n + 3))
                    nc.scalar.copy(qsplit[:, :, 0:2, :], twice(qrot)).then_inc(qhi_ok, 1)

            over_sequences(step)(act)

            act.wait_ge(gap_ok, 1)
            nc.scalar.activation(ratio[:, :], gap[:, :], ACT.Exp).then_inc(ratio_ok, 1)

            act.wait_ge(experts_ok, 1)
            act.wait_ge(w1lo_ok, B)
            act.wait_ge(w2lo_ok, B)

            def step_c(tile):
                t, one = tile[0], tile[3]
                n = P if one else ROWS
                e = act.value_load(tile_expert[0:1, bass.ds(t, 1)], min_val=0, max_val=E - 1)
                for pair in range(4):
                    act.wait_ge(h_made, 4 * t + pair + 1)
                    if tile_exists(shift(tile, -1)):
                        act.wait_ge(glo_ok, 4 * t + pair - 3)
                    for c in (2 * pair, 2 * pair + 1):
                        last = nc.scalar.activation(act32[:, c * ROWS:c * ROWS + n],
                                                    h_ps[pair][:, c % 2 * ROWS:c % 2 * ROWS + n],
                                                    ACT.Gelu, bias=b1c[:, bass.ds(e * HC + c, 1)])
                    last.then_inc(gelu_ok, 1)

            over_tiles(act, step_c)

        @block.vector
        def _(dve):
            dve.wait_ge(const_in, 48)
            dve.wait_ge(gates_ready, 1)

            def stats_first(i, n):
                dve.wait_ge(xc_in[n % SLOTS], 32 * (i + n // SLOTS + 1))
                nc.vector.bn_stats(stats[:, :], xin[n % SLOTS]).then_inc(stats1_ok, 1)

            def moments_first(i, n):
                own(dve, stats1_ok, num(i, n + 1))
                nc.vector.bn_aggr(mean1, stats[:, :]).then_inc(mean1_ok, 1)

            def stats_second(i, n):
                dve.wait_ge(x1_ok, num(i, n + 1))
                nc.vector.bn_stats(stats2[:, :], xin[n % SLOTS]).then_inc(stats2_ok, 1)

            def moments_second(i, n):
                own(dve, stats2_ok, num(i, n + 1))
                nc.vector.bn_aggr(mean2, stats2[:, :]).then_inc(mean2_ok, 1)

            def rotary_k_terms(i, n):
                s = n % SLOTS
                if real(i, n - 1):
                    dve.wait_ge(k_ok, num(i, n))
                nc.vector.tensor_tensor(krot, cin[s], cst[:, CK:CK + D], ALU.mult).then_inc(kterms, 1)
                nc.vector.tensor_tensor(pairs(kturn), swapped(cin[s]), pairs(cst[:, SK:SK + D]),
                                        ALU.mult).then_inc(kterms, 1)

            def rotary_k(i, n):
                dve.wait_ge(kterms, 2 * num(i, n + 1))
                nc.vector.tensor_tensor(krot, krot, kturn, ALU.add).then_inc(krot_ok, 1)

            def normalise_first(i, n):
                dve.wait_ge(rstd_ok, num(i, n + 1))
                nc.vector.tensor_scalar(xn, xin[n % SLOTS], mean1[:, 0:1], rstd[:, 0:1],
                                        ALU.subtract, ALU.mult).then_inc(xn_ok, 1)

            def rotary_q_terms(i, n):
                dve.wait_ge(xn_ok, num(i, n + 1))
                nc.vector.tensor_tensor(qrot, xn, cst[:, CQ:CQ + D], ALU.mult).then_inc(qterms, 1)
                nc.vector.tensor_tensor(pairs(turn), swapped(xn), pairs(cst[:, SQ:SQ + D]),
                                        ALU.mult).then_inc(qterms, 1)

            def rotary_q(i, n):
                dve.wait_ge(qterms, 2 * num(i, n + 1))
                nc.vector.tensor_tensor(qrot, qrot, turn, ALU.add).then_inc(qrot_ok, 1)

            def low_q(i, n):
                dve.wait_ge(qhi_ok, num(i, n + 1))
                nc.vector.tensor_tensor(qsplit[:, :, 2:4, :], twice(qrot), qsplit[:, :, 0:2, :],
                                        ALU.subtract).then_inc(q_ok, 1)

            def first_residual(i, n):
                dve.wait_ge(out_made, num(i, n + 1))
                by_head = xin[n % SLOTS].rearrange("p (h d) -> p h d", d=HD)
                nc.vector.scalar_tensor_tensor(
                    out=by_head, in0=o_ps[:, :].rearrange("p (h d) -> p h d", d=32)[:, :, 0:HD],
                    scalar=gate[:, 0:1], in1=by_head, op0=ALU.mult, op1=ALU.add).then_inc(x1_ok, 1)

            def mask_bank_0(i, n):
                dve.wait_ge(score_made, 4 * num(i, n) + 4)
                nc.vector.tensor_tensor(smask[0], sc_ps[0][:, :].rearrange("p (g n) -> p g n", g=4),
                                        cst[:, CAUSAL:CAUSAL + P].unsqueeze(1).to_broadcast([P, 4, P]),
                                        ALU.mult).then_inc(s0_ok, 1)

            def split_w1(i, n):
                dve.wait_ge(w1hi_ok, num(i, n + 1))
                at = w1_at(i, n)
                nc.vector.tensor_tensor(w1s[:, bass.ds(at + DC * H, H)], raw1[n % 2], w1s[:, bass.ds(at, H)],
                                        ALU.subtract).then_inc(w1lo_ok, 1)

            def keep_logits(i, n):
                dve.wait_ge(logit_made, num(i, n + 1))
                nc.vector.tensor_copy(logits[:, bass.ds(num(i, n) * E, E)], logit_ps).then_inc(logit_ok, 1)

            def normalise_second(i, n):
                dve.wait_ge(rstd_ok, num(i, n + 4))
                if real(i, n - 1):
                    dve.wait_ge(x2T_made, num(i, n))
                nc.vector.tensor_scalar(x2n[:, :], xin[n % SLOTS], mean2[:, 0:1], rstd[:, 1:2],
                                        ALU.subtract, ALU.mult).then_inc(x2n_ok, 1)

            def low_second(i, n):
                dve.wait_ge(x2hi_ok, num(i, n + 1))
                nc.vector.tensor_tensor(x2split[n % SLOTS][:, D:2 * D], x2n[:, :], x2split[n % SLOTS][:, 0:D],
                                        ALU.subtract).then_inc(x2lo_ok, 1)

            def step(i, n):
                if real(i, n - 1):
                    first_residual(i, n - 1)
                    stats_second(i, n - 1)
                if real(i, n + 2):
                    stats_first(i, n + 2)
                if real(i, n):
                    mask_bank_0(i, n)
                if real(i, n + 2):
                    rotary_k_terms(i, n + 2)
                if real(i, n - 1):
                    moments_second(i, n - 1)
                if real(i, n + 2):
                    moments_first(i, n + 2)
                    rotary_k(i, n + 2)
                if real(i, n - 2):
                    keep_logits(i, n - 2)
                if real(i, n - 1):
                    normalise_second(i, n - 1)
                if real(i, n + 2):
                    normalise_first(i, n + 2)
                    rotary_q_terms(i, n + 2)
                    rotary_q(i, n + 2)
                if real(i, n):
                    split_w1(i, n)
                if real(i, n - 1):
                    low_second(i, n - 1)
                if real(i, n + 2):
                    low_q(i, n + 2)

            over_sequences(step)(dve)

            steps = 0

            def then(ins):
                nonlocal steps
                steps += 1
                ins.then_inc(route_step, 1)
                dve.wait_ge(route_step, steps)

            def by_sequence(ap):
                return ap.rearrange("p (b e) -> p b e", e=E)

            def over_experts(ap):
                return ap.unsqueeze(2).to_broadcast([P, B, E])

            below8 = cst[:, BELOW8:BELOW8 + E].unsqueeze(1).to_broadcast([P, B, E])
            dve.wait_ge(logit_ok, B)
            for choice in range(TOPK):
                left = logits if choice == 0 else others
                then(nc.vector.tensor_reduce(best[:, choice, :], by_sequence(left[:, :]), AX.X, ALU.max))
                then(nc.vector.tensor_tensor(by_sequence(ties[:, :]), by_sequence(left[:, :]),
                                             over_experts(best[:, choice, :]), ALU.is_equal))
                then(nc.vector.tensor_tensor(by_sequence(ties[:, :]), by_sequence(ties[:, :]), below8, ALU.mult))
                then(nc.vector.tensor_reduce(first[:, :], by_sequence(ties[:, :]), AX.X, ALU.min))
                then(nc.vector.tensor_tensor(onehot[:, choice, :, :], below8, over_experts(first[:, :]),
                                             ALU.is_equal))
                if choice == 0:
                    then(nc.vector.scalar_tensor_tensor(
                        out=others[:, :], in0=onehot[:, 0, :, :].rearrange("p b e -> p (b e)"), scalar=-3e38,
                        in1=logits[:, :], op0=ALU.mult, op1=ALU.add))
            nc.vector.tensor_tensor(gap[:, :], best[:, 1, :], best[:, 0, :], ALU.subtract).then_inc(gap_ok, 1)
            nc.vector.memset(chosen[:, B, :], 0.0).then_inc(chosen_ok, 1)
            nc.vector.tensor_tensor(chosen[:, 0:B, :], onehot[:, 0, :, :], onehot[:, 1, :, :],
                                    ALU.add).then_inc(chosen_ok, 1)
            dve.wait_ge(ratio_ok, 1)
            then(nc.vector.tensor_scalar(total[:, :], ratio[:, :], 1.0, None, ALU.add))
            then(nc.vector.reciprocal(inverse[:, :], total[:, :]))
            then(nc.vector.tensor_scalar(weight[:, 0:B], inverse[:, :], gate[:, 1:2], None, ALU.mult))
            then(nc.vector.tensor_tensor(weight[:, B:2 * B], weight[:, 0:B], ratio[:, :], ALU.mult))
            dve.wait_ge(rank_made, 1)
            then(nc.vector.tensor_scalar(count_i[:, :], rank_ps[:, B * E:(B + 1) * E], float(P - 1), None, ALU.add))
            nc.vector.tensor_scalar(parts_i[:, 0, :], count_i[:, :], 7, None, ALU.arith_shift_right)
            then(nc.vector.tensor_scalar(parts_i[:, 1, :], count_i[:, :], 8, None, ALU.arith_shift_right))
            then(nc.vector.tensor_copy(parts_f[:, :, :], parts_i[:, :, :]))
            then(nc.vector.tensor_tensor_scan(pair_end[:, :], twos, twos, 0.0, ALU.add, ALU.bypass))
            then(nc.vector.tensor_tensor(pair_start[:, :], pair_end[:, :], twos, ALU.subtract))
            then(nc.vector.tensor_scalar(pair_end[:, :], pair_end[:, :], float(PAIRS), None, ALU.min))
            then(nc.vector.tensor_scalar(pair_start[:, :], pair_start[:, :], float(PAIRS), None, ALU.min))
            then(nc.vector.tensor_tensor(paired[:, :], pair_end[:, :], pair_start[:, :], ALU.subtract))
            nc.vector.tensor_scalar(wide_base[:, :], pair_start[:, :], float(ROWS), None, ALU.mult)
            nc.vector.tensor_scalar(wide_rows[:, :], paired[:, :], float(ROWS), None, ALU.mult)
            then(nc.vector.scalar_tensor_tensor(out=single[:, :], in0=paired[:, :], scalar=-2.0, in1=units,
                                                op0=ALU.mult, op1=ALU.add))
            then(nc.vector.tensor_tensor_scan(single_end[:, :], single[:, :], single[:, :], 0.0, ALU.add, ALU.bypass))
            then(nc.vector.tensor_tensor(single_start[:, :], single_end[:, :], single[:, :], ALU.subtract))
            then(nc.vector.tensor_scalar(jump[:, :], single_start[:, :], float(2 * PAIRS), float(P), ALU.add, ALU.mult))
            then(nc.vector.tensor_tensor(jump[:, :], jump[:, :], wide_rows[:, :], ALU.subtract))
            then(nc.vector.tensor_tensor(jump[:, :], jump[:, :], wide_base[:, :], ALU.subtract))
            def each(ap):
                return ap.unsqueeze(1).to_broadcast([P, B, E])

            rank = rank_ps[:, 0:B * E].rearrange("p (b e) -> p b e", e=E)
            then(nc.vector.tensor_tensor(beyond[:, :, :], rank, each(wide_rows[:, :]), ALU.is_ge))
            nc.vector.tensor_tensor(slot[:, :, :], rank, each(wide_base[:, :]), ALU.add)
            then(nc.vector.tensor_tensor(beyond[:, :, :], beyond[:, :, :], each(jump[:, :]), ALU.mult))
            then(nc.vector.tensor_tensor(slot[:, :, :], slot[:, :, :], beyond[:, :, :], ALU.add))
            for choice in range(TOPK):
                then(nc.vector.tensor_tensor(slot_k[:, choice, :, :], onehot[:, choice, :, :], slot[:, :, :],
                                             ALU.mult))
            then(nc.vector.tensor_reduce(slots[:, :], slot_k[:, :, :, :].rearrange("p k b e -> p (k b) e"),
                                         AX.X, ALU.add))
            then(nc.vector.tensor_copy(slots_i[:, :], slots[:, :]))
            then(nc.vector.tensor_scalar(tile_i[:, :], slots_i[:, :], 7, None, ALU.arith_shift_right))
            then(nc.vector.tensor_copy(tile_f[:, :], tile_i[:, :]))
            nc.vector.scalar_tensor_tensor(out=lane_f[:, :], in0=tile_f[:, :], scalar=-float(P),
                                           in1=slots[:, :], op0=ALU.mult, op1=ALU.add).then_inc(lanes_ok, 1)

            def onto(ap, width):
                return ap.unsqueeze(2).to_broadcast([P, HOT, width])

            for c in range(HOTS):
                columns = slice(c * HOT, (c + 1) * HOT)
                if c >= 2:
                    dve.wait_ge(weight_hot_ok, c - 1)
                nc.vector.tensor_tensor(tile_eq[c % 2],
                                        cst[:, IOTA:IOTA + TCOLS].unsqueeze(1).to_broadcast([P, HOT, TCOLS]),
                                        onto(tile_f[:, columns], TCOLS), ALU.is_equal).then_inc(tile_eq_ok, 1)
                token = TOKEN1 + c * HOT % B
                dve.wait_ge(tile_eq_ok, c + 1)
                nc.vector.tensor_tensor(tile_hot[c][:, :, 0, :], tile_eq[c % 2], onto(cst[:, token:token + HOT], TCOLS),
                                        ALU.mult).then_inc(token_hot_ok, 1)
                if c == 0:
                    dve.wait_ge(lanes_ok, 1)
                nc.vector.tensor_tensor(lane_hot[c], cst[:, IOTA:IOTA + P].unsqueeze(1).to_broadcast([P, HOT, P]),
                                        onto(lane_f[:, columns], P), ALU.is_equal).then_inc(lane_hot_ok, 1)

            def ended(first, count, ends):
                return nc.vector.tensor_tensor(
                    tile_ge[:, first:first + count, :],
                    cst[0:1, IOTA:IOTA + count].unsqueeze(2).to_broadcast([1, count, E]),
                    ends[0:1, :].unsqueeze(1).to_broadcast([1, count, E]), ALU.is_ge)

            ended(0, PAIRS, pair_end)
            then(ended(PAIRS, SINGLES, single_end))
            then(nc.vector.tensor_reduce(tile_exp[:, :], tile_ge[:, :, :], AX.X, ALU.add))
            nc.vector.tensor_scalar(tile_expert[:, :], tile_exp[:, :], float(E - 1), None,
                                    ALU.min).then_inc(experts_ok, 1)
            dve.wait_ge(hot_used, HOTS)
            then(nc.vector.tensor_copy(table[:, :, :], table_ps[:, 0:2 * TCOLS]))
            then(nc.vector.tensor_scalar(row_less1[:, :], table[:, 0, :], -1.0, None, ALU.add))
            then(nc.vector.tensor_scalar(empty[:, :], table[:, 0, :], 0.0, cst[:, SPARE1:SPARE1 + 1],
                                         ALU.is_equal, ALU.mult))
            nc.vector.tensor_scalar(gather_row[:, :], row_less1[:, :], 0.0, None, ALU.max).then_inc(slots_ok, 1)
            nc.vector.tensor_tensor(scatter_row[:, :], row_less1[:, :], empty[:, :], ALU.add).then_inc(slots_ok, 1)

            def rows_transposed(tile):
                t, k, par, one = tile
                n = P if one else ROWS
                dve.wait_ge(rowsT_made, t + 1)
                nc.vector.tensor_copy(rowsT[par].rearrange("p s c n -> p (s c) n")[:, :, 0:n],
                                      t_ps[:, 0:4 * ROWS].rearrange("p (s n) -> p s n", s=4)[:, :, 0:n]
                                      ).then_inc(rowsT_ok, 1)

            dve.wait_ge(b2_in, 16)
            dve.wait_ge(experts_ok, 1)
            rows_transposed((0, 0, 0, False))

            def split(tile, pair):
                t, k, par, one = tile
                n = P if one else ROWS
                c = slice(2 * pair, 2 * pair + 2)
                piece = act32[:, 2 * pair * ROWS:2 * (pair + 1) * ROWS].rearrange("p (c n) -> p c n", c=2)[:, :, 0:n]
                dve.wait_ge(gelu_ok, 4 * t + pair + 1)
                nc.vector.tensor_copy(ghi[par][:, c, 0:n], piece).then_inc(ghi_ok, 1)
                dve.wait_ge(ghi_ok, 4 * t + pair + 1)
                nc.vector.tensor_tensor(glo[par][:, c, 0:n], piece, ghi[par][:, c, 0:n],
                                        ALU.subtract).then_inc(glo_ok, 1)

            def weigh(tile):
                t = tile[0]
                e = dve.value_load(tile_expert[0:1, bass.ds(t, 1)], min_val=0, max_val=E - 1)
                if tile_exists(shift(tile, -1)):
                    dve.wait_ge(yout_ok, parts(tile)[0][0])
                dve.wait_ge(y_made, t + 1)
                for unit, side, k in parts(tile):
                    nc.vector.tensor_tensor(ysum[side], y_ps[side][:, 0:D], b2bc[:, bass.ds(e * D, D)],
                                            ALU.add).then_inc(ybias_ok, 1)
                for unit, side, k in parts(tile):
                    dve.wait_ge(ybias_ok, unit + 1)
                    nc.vector.tensor_tensor(ysum[side], y_ps[side][:, D:2 * D], ysum[side],
                                            ALU.add).then_inc(ysum_ok, 1)
                for unit, side, k in parts(tile):
                    dve.wait_ge(ysum_ok, unit + 1)
                    if not (isinstance(unit, int) and unit < 2):
                        dve.wait_ge(scattered[side], 16 * k)
                    nc.vector.tensor_scalar(yout[side], ysum[side], slot_gate[:, bass.ds(unit, 1)],
                                            None, ALU.mult).then_inc(yout_ok, 1)

            def step_c(tile):
                for pair in range(4):
                    split(tile, pair)
                    if pair == 2 and tile_exists(shift(tile, 1)):
                        rows_transposed(shift(tile, 1))
                if tile_exists(shift(tile, -1)):
                    weigh(shift(tile, -1))

            over_tiles(dve, step_c)
            weigh((TILES - 1, (TILES - 1) // 2, (TILES - 1) % 2, True))

        @block.tensor
        def _(pe):
            pe.wait_ge(const_in, 48)
            pe.wait_ge(halves_ok, 1)
            pe.wait_ge(pads_set, 1)
            identity_b = cstb[:, IDENT_B:IDENT_B + P]

            def transpose_kq(i, n):
                for source, to, ready, made, copied_out in ((ksplit, kT_ps, k_ok, kT_made, kT_ok),
                                                            (qsplit, qT_ps, q_ok, qT_made, qT_ok)):
                    if real(i, n - 1):
                        pe.wait_ge(copied_out, num(i, n))
                    pe.wait_ge(ready, num(i, n + 1))
                    for g in range(HEADS // 2):
                        last = nc.tensor.transpose(to[:, g * P:(g + 1) * P],
                                                   source[:, 2 * g:2 * g + 2, :, :].rearrange("p h s d -> p (h s d)"),
                                                   identity_b)
                    last.then_inc(made, 1)

            def scores(i, n, which):
                t = num(i, n)
                pe.wait_ge(kT_ok, t + 1)
                pe.wait_ge(qT_ok, t + 1)
                for j in which:
                    rows = slice(64 * (j % 2), 64 * (j % 2) + 64)
                    if real(i, n - 1):
                        if j == 0:
                            pe.wait_ge(outT_ok, t)
                        else:
                            pe.wait_ge(copied, 3 * t + j - 3)
                    for g in range(4):
                        at = j // 2 * 4 + g
                        last = nc.tensor.matmul(sc_ps[j][:, g * P:(g + 1) * P], kT[rows, at, :], qT[rows, at, :],
                                                start=True, stop=True)
                    last.then_inc(score_made, 1)

            def values(i, n):
                t = num(i, n)
                pe.wait_ge(s0_ok, t + 1)
                pe.wait_ge(selected, 3 * t + 3)
                for h in range(HEADS):
                    at, column = h // 4, 32 * (h % 4)
                    last = nc.tensor.matmul(outT_ps[column:column + 32, at * P:(at + 1) * P],
                                            context[:, n % SLOTS, h * HD:h * HD + 32],
                                            smask[h // 8 * 2 + h % 2][:, h % 8 // 2, :], start=True, stop=True)
                last.then_inc(outT_made, 1)

            def transpose_outputs(i, n):
                pe.wait_ge(outT_ok, num(i, n + 1))
                if real(i, n - 1):
                    pe.wait_ge(x1_ok, num(i, n))
                for j in range(4):
                    last = nc.tensor.transpose(o_ps[:, j * P:(j + 1) * P], outT[:, j * P:(j + 1) * P],
                                               cst[:, IDENT:IDENT + P])
                last.then_inc(out_made, 1)

            def transpose_normed(i, n):
                pe.wait_ge(x2n_ok, num(i, n + 1))
                for d in range(DC):
                    last = nc.tensor.transpose(r_ps[:, d * P:(d + 1) * P], x2n[:, d * P:(d + 1) * P],
                                               cst[:, IDENT:IDENT + P])
                last.then_inc(x2T_made, 1)

            def router(i, n):
                pe.wait_ge(x2T_ok, num(i, n + 1))
                for d in range(DC):
                    last = nc.tensor.matmul(logit_ps, x2T[:, d, :], rw[:, d, :],
                                            start=(d == 0), stop=(d == DC - 1))
                last.then_inc(logit_made, 1)

            def step(i, n):
                if real(i, n):
                    scores(i, n, (1, 2, 3))
                if real(i, n - 1):
                    transpose_outputs(i, n - 1)
                if real(i, n):
                    scores(i, n, (0,))
                if real(i, n - 2):
                    transpose_normed(i, n - 2)
                if real(i, n + 1):
                    transpose_kq(i, n + 1)
                if real(i, n - 2):
                    router(i, n - 2)
                if real(i, n):
                    values(i, n)

            over_sequences(step)(pe)

            pe.wait_ge(chosen_ok, 2)
            for ahead in range(1, B + 1):
                nc.tensor.matmul(rank_ps[:, ahead * E:(B + 1) * E], cstb[:, ONES_B:ONES_B + P],
                                 chosen[:, 0:B + 1 - ahead, :].rearrange("p b e -> p (b e)"),
                                 start=(ahead == 1), stop=False, skip_group_check=True)
            last = nc.tensor.matmul(rank_ps[:, 0:(B + 1) * E], cstb[:, BEFORE_B:BEFORE_B + P],
                                    chosen[:, :, :].rearrange("p b e -> p (b e)"),
                                    start=False, stop=True, skip_group_check=True)
            last.then_inc(rank_made, 1)

            for c in range(HOTS):
                pe.wait_ge(token_hot_ok, c + 1)
                pe.wait_ge(weight_hot_ok, c + 1)
                pe.wait_ge(lane_hot_ok, c + 1)
                for n in range(HOT):
                    last = nc.tensor.matmul(table_ps[:, 0:2 * TCOLS], lane_hot[c][:, n, :],
                                            tile_hot[c][:, n, :, :].rearrange("p a l -> p (a l)"),
                                            start=(c == 0 and n == 0), stop=(c == HOTS - 1 and n == HOT - 1))
                last.then_inc(hot_used, 1)

            def transpose_rows(tile):
                t, k, par, one = tile
                pe.wait_ge(gathered[par], 16 * units_of_parity_through(tile))
                if tile_exists(shift(tile, -1)):
                    pe.wait_ge(rowsT_ok, t)
                for n in range(4):
                    for half in range(len(parts(tile))):
                        at = n * ROWS + half * P
                        last = nc.tensor.transpose(t_ps[:, at:at + P], rows_in[par][:, half, n * P:(n + 1) * P],
                                                   identity_b)
                last.then_inc(rowsT_made, 1)

            def hidden(tile, e):
                t, k, par, one = tile
                rows = P if one else ROWS
                pe.wait_ge(rowsT_ok, t + 1)
                if tile_exists(shift(tile, -1)):
                    pe.wait_ge(gelu_ok, 4 * t)
                for c in range(HC):
                    n = 0
                    for wpart, xpart in ((0, 0), (0, 1), (1, 0)):
                        for d in range(DC):
                            last = nc.tensor.matmul(
                                h_ps[c // 2][:, c % 2 * ROWS:c % 2 * ROWS + rows],
                                w1s[:, bass.ds(e * (2 * DC * H) + (wpart * DC + d) * H + c * P, P)],
                                rowsT[par][:, xpart, d, 0:rows], start=(n == 0), stop=(n == 3 * DC - 1))
                            n += 1
                    if c % 2 == 1:
                        last.then_inc(h_made, 1)

            def output(tile, e):
                t, k, par, one = tile
                if tile_exists(shift(tile, -1)):
                    pe.wait_ge(ysum_ok, parts(tile)[0][0] - (1 if one else 0))
                if tile_exists(shift(tile, 1)):
                    pe.wait_ge(glo_ok, 4 * t + 4)
                for c in range(HC):
                    if c % 2 == 0 and not tile_exists(shift(tile, 1)):
                        pe.wait_ge(glo_ok, 4 * t + c // 2 + 1)
                    base = e * (2 * HC * D) + c * (2 * D)
                    for half, (unit, side, _) in enumerate(parts(tile)):
                        rows = slice(half * P, (half + 1) * P)
                        for low in ((True, False) if c == HC - 1 else (False, True)):
                            columns = D if low else 2 * D
                            last = nc.tensor.matmul(y_ps[side][:, 0:columns], (glo if low else ghi)[par][:, c, rows],
                                                    w2s[:, bass.ds(base, columns)],
                                                    start=(c == 0 and not low), stop=(c == HC - 1 and not low))
                last.then_inc(y_made, 1)

            known = {}

            def key(tile):
                return tile[0] if isinstance(tile[0], int) else tile[2]

            def load_expert(tile):
                return pe.value_load(tile_expert[0:1, bass.ds(tile[0], 1)], min_val=0, max_val=E - 1)

            pe.wait_ge(experts_ok, 1)
            pe.wait_ge(w1lo_ok, B)
            pe.wait_ge(w2lo_ok, B)
            start = (0, 0, 0, False)
            transpose_rows(start)
            e = known[key(start)] = load_expert(start)
            hidden(start, e)
            transpose_rows(shift(start, 1))

            def step_c(tile):
                follower = shift(tile, 1)
                e = known.pop(key(tile)) if key(tile) in known else load_expert(tile)
                if tile_exists(follower):
                    next_e = known[key(follower)] = load_expert(follower)
                    hidden(follower, next_e)
                if tile_exists(shift(tile, 2)):
                    transpose_rows(shift(tile, 2))
                output(tile, e)

            over_tiles(pe, step_c, at_bounds=known.clear)


def kernel(x, ctx_1024, g_xattn, g_ffn, L0_ffn_router_w, L0_ffn_w1, L0_ffn_b1, L0_ffn_w2, L0_ffn_b2):
    import concourse.bacc as bacc
    from concourse.bass_utils import run_bass_kernel_spmd

    const, const_b = constants()
    arrays = {
        "x_in": np.ascontiguousarray(x),
        "ctx_in": np.ascontiguousarray(ctx_1024),
        "gates_in_": np.concatenate([np.asarray(g_xattn), np.asarray(g_ffn)]).reshape(1, 2),
        "router_in": np.ascontiguousarray(L0_ffn_router_w),
        "w1_in": np.ascontiguousarray(L0_ffn_w1),
        "b1_in": np.ascontiguousarray(np.asarray(L0_ffn_b1).reshape(E * HC, P).T),
        "w2_in": np.ascontiguousarray(L0_ffn_w2),
        "b2_in_": np.ascontiguousarray(np.asarray(L0_ffn_b2).reshape(1, E * D)),
        "const_in_": const,
        "const_b_in_": const_b,
    }
    nc = bacc.Bacc("TRN2", target_bir_lowering=False, num_devices=1)
    args = [nc.dram_tensor(n, a.shape, mybir.dt.from_np(a.dtype), kind="ExternalInput").ap() for n, a in arrays.items()]
    out = nc.dram_tensor("out_rows", [TOKENS + SPARE, D], F32, kind="ExternalOutput").ap()
    build(nc, *args, out)
    result = run_bass_kernel_spmd(nc, [arrays], core_ids=[0])
    return result.results[0]["out_rows"][:TOKENS].reshape(B, S, D)
```
